# Optimizing a Trainium2 kernel written in Bass

```python
import numpy as np
import jax
import jax.numpy as jnp

def _softmax(x, axis=-1):
    return jax.nn.softmax(x, axis=axis)

def _gelu(x):
    return jax.nn.gelu(x, approximate=True)

def _silu(x):
    return jax.nn.silu(x)

def _sigmoid(x):
    return jax.nn.sigmoid(x)

def _layernorm(x, axis=-1, eps=1e-05):
    m = jnp.mean(x, axis=axis, keepdims=True)
    v = jnp.var(x, axis=axis, keepdims=True)
    return (x - m) / jnp.sqrt(v + eps)

def _scatter_add(tgt, idx, src, axis=0):
    return tgt.at[idx].add(src)

def _segment_sum(src, seg, n):
    return jax.ops.segment_sum(src, seg, n)
kernel_name = 'mk_gnn_preln_d2_gnn_r8_89271d'

def setup_inputs(seed: int=0):
    np.random.seed(seed)
    _w = jnp.asarray

    def _rec_inputs():
        import jax
        import jax.numpy as jnp
        _gk = jax.random.key(seed)
        x = -8.776e-05 + 1 * jax.random.normal(jax.random.fold_in(_gk, 1), (1250, 512), jnp.float32)
        src = jax.random.randint(jax.random.fold_in(_gk, 2), (20000,), 0, 1250, jnp.int32)
        dst = jax.random.randint(jax.random.fold_in(_gk, 3), (20000,), 0, 1250, jnp.int32)
        _o = jnp.argsort(dst, stable=True)
        src = src[_o]
        dst = dst[_o]
        return (x, src, dst)
    x, src, dst = _rec_inputs()

    def _L0_gnn_setup():
        import jax, jax.numpy as jnp
        import numpy as np
        N_NODES = 1250
        IN_F = 512
        OUT_F = 512
        N_EDGES = 20000
        GRID_SIZE = 5
        SPLINE_ORDER = 3
        ALPHA = 0.2

        def _grid():
            step = 2.0 / GRID_SIZE
            return jnp.arange(-SPLINE_ORDER, GRID_SIZE + SPLINE_ORDER + 1, dtype=jnp.float32) * step - 1.0

        def _b_splines(x, grid):
            x = x[..., None]
            bases = ((x >= grid[:-1]) & (x < grid[1:])).astype(x.dtype)
            for p in range(1, SPLINE_ORDER + 1):
                left = (x - grid[:-(p + 1)]) / (grid[p:-1] - grid[:-(p + 1)]) * bases[..., :-1]
                right = (grid[p + 1:] - x) / (grid[p + 1:] - grid[1:-p]) * bases[..., 1:]
                bases = left + right
            return bases
        key = jax.random.key(seed)
        k1, k2, k3, k4, k5, k6 = jax.random.split(key, 6)
        h = jax.random.normal(k1, (N_NODES, IN_F), dtype=jnp.float32)
        edge_index = jax.random.randint(k2, (2, N_EDGES), 0, N_NODES, dtype=jnp.int64)
        xav = float(np.sqrt(2.0 / (IN_F + OUT_F))) * 1.414
        W = jax.random.normal(k3, (IN_F, OUT_F), dtype=jnp.float32) * xav
        a = jax.random.normal(k4, (2 * OUT_F, 1), dtype=jnp.float32) * float(np.sqrt(2.0 / (2 * OUT_F + 1)))
        base_w = jax.random.normal(k5, (OUT_F, IN_F), dtype=jnp.float32) * xav
        n_coef = GRID_SIZE + SPLINE_ORDER
        spline_w = jax.random.normal(k6, (OUT_F, IN_F, n_coef), dtype=jnp.float32) * 0.1
        return {'h': h, 'W': W, 'a': a, 'base_w': base_w, 'spline_w': spline_w, 'edge_index': edge_index}
    _L0_gnn_all = _L0_gnn_setup()
    _L0_gnn_in = {k: v for k, v in _L0_gnn_all.items() if k in ('W', 'a', 'base_w', 'spline_w')}
    del _L0_gnn_all

    def _L1_gnn_setup():
        import jax, jax.numpy as jnp
        import numpy as np
        BN_EPS = 1e-05
        N_NODES, N_EDGES, D, N_LAYERS = (6250, 50000, 512, 3)
        key = jax.random.key(seed)
        k_x, k_e, k_w = jax.random.split(key, 3)
        x = jax.random.normal(k_x, (N_NODES, D), dtype=jnp.float32)
        edge_index = jax.random.randint(k_e, (2, N_EDGES), 0, N_NODES, dtype=jnp.int64)
        W = jax.random.normal(k_w, (N_LAYERS, D, D), dtype=jnp.float32) * (1.0 / np.sqrt(D))
        b = jnp.zeros((N_LAYERS, D), dtype=jnp.float32)
        gamma = jnp.ones((N_LAYERS, D), dtype=jnp.float32)
        beta = jnp.zeros((N_LAYERS, D), dtype=jnp.float32)
        return {'x': x, 'edge_index': edge_index, 'W': W, 'b': b, 'gamma': gamma, 'beta': beta}
    _L1_gnn_all = _L1_gnn_setup()
    _L1_gnn_in = {k: v for k, v in _L1_gnn_all.items() if k in ('W', 'b', 'gamma', 'beta')}
    del _L1_gnn_all
    return {'x': x, 'src': src, 'dst': dst, 'L0_gnn_W': _L0_gnn_in['W'], 'L0_gnn_a': _L0_gnn_in['a'], 'L0_gnn_base_w': _L0_gnn_in['base_w'], 'L0_gnn_spline_w': _L0_gnn_in['spline_w'], 'L1_gnn_W': _L1_gnn_in['W'], 'L1_gnn_b': _L1_gnn_in['b'], 'L1_gnn_gamma': _L1_gnn_in['gamma'], 'L1_gnn_beta': _L1_gnn_in['beta']}

def reference(x, src, dst, L0_gnn_W, L0_gnn_a, L0_gnn_base_w, L0_gnn_spline_w, L1_gnn_W, L1_gnn_b, L1_gnn_gamma, L1_gnn_beta):
    import jax
    import jax.numpy as jnp

    def _L0_gnn_ref(h, W, a, base_w, spline_w, edge_index):
        import jax, jax.numpy as jnp
        import numpy as np
        N_NODES = 1250
        IN_F = 512
        OUT_F = 512
        N_EDGES = 20000
        GRID_SIZE = 5
        SPLINE_ORDER = 3
        ALPHA = 0.2

        def _grid():
            step = 2.0 / GRID_SIZE
            return jnp.arange(-SPLINE_ORDER, GRID_SIZE + SPLINE_ORDER + 1, dtype=jnp.float32) * step - 1.0

        def _b_splines(x, grid):
            x = x[..., None]
            bases = ((x >= grid[:-1]) & (x < grid[1:])).astype(x.dtype)
            for p in range(1, SPLINE_ORDER + 1):
                left = (x - grid[:-(p + 1)]) / (grid[p:-1] - grid[:-(p + 1)]) * bases[..., :-1]
                right = (grid[p + 1:] - x) / (grid[p + 1:] - grid[1:-p]) * bases[..., 1:]
                bases = left + right
            return bases
        HW = h @ W
        row, col = (edge_index[0], edge_index[1])
        s = HW @ a[:OUT_F, 0]
        t = HW @ a[OUT_F:, 0]
        e = jax.nn.leaky_relu(s[row] + t[col], negative_slope=ALPHA)
        m = jax.ops.segment_max(e, row, num_segments=N_NODES)
        ex = jnp.exp(e - m[row])
        den = jax.ops.segment_sum(ex, row, num_segments=N_NODES)
        att = ex / den[row]
        agg = jax.ops.segment_sum(att[:, None] * h[col], row, num_segments=N_NODES)
        grid = _grid()
        basis = _b_splines(agg, grid)
        out = jax.nn.silu(agg) @ base_w.T + jnp.einsum('nip,oip->no', basis, spline_w)
        return out

    def _L1_gnn_ref(x, W, b, gamma, beta, edge_index):
        import jax, jax.numpy as jnp
        import numpy as np
        BN_EPS = 1e-05
        N_NODES, N_EDGES, D, N_LAYERS = (6250, 50000, 512, 3)
        N = x.shape[0]
        loops = jnp.arange(N, dtype=edge_index.dtype)
        src = jnp.concatenate([edge_index[0], loops])
        dst = jnp.concatenate([edge_index[1], loops])
        deg = jax.ops.segment_sum(jnp.ones(src.shape, jnp.float32), dst, num_segments=N)
        dinv = jax.lax.rsqrt(deg)
        norm = dinv[src] * dinv[dst]
        for l in range(W.shape[0]):
            h = x @ W[l].T
            agg = jax.ops.segment_sum(h[src] * norm[:, None], dst, num_segments=N) + b[l]
            mean = jnp.mean(agg, axis=0)
            var = jnp.mean((agg - mean) ** 2, axis=0)
            xn = (agg - mean) * jax.lax.rsqrt(var + BN_EPS)
            x = jax.nn.relu(gamma[l] * xn + beta[l])
        return x
    edge_index = jnp.stack([src, dst])
    h = jnp.maximum(_layernorm(x, axis=-1), 0.0)
    x = x + _L0_gnn_ref(h, L0_gnn_W, L0_gnn_a, L0_gnn_base_w, L0_gnn_spline_w, edge_index)
    h = jnp.maximum(_layernorm(x, axis=-1), 0.0)
    x = x + _L1_gnn_ref(h, L1_gnn_W, L1_gnn_b, L1_gnn_gamma, L1_gnn_beta, edge_index)
    return x

_drawn_inputs = setup_inputs


def setup_inputs(seed=0):
    import zlib

    import numpy as np

    out = dict(_drawn_inputs(seed))
    spreads = {'L1_gnn_b': (0.0, 0.1), 'L1_gnn_gamma': (1.0, 0.2), 'L1_gnn_beta': (0.0, 0.1)}
    factors = {}
    for name, (base, spread) in spreads.items():
        noise = np.random.default_rng([zlib.crc32(name.encode()), seed]).standard_normal(out[name].shape)
        drawn = base * np.exp(spread * noise) if base else spread * noise
        out[name] = jnp.asarray(drawn.astype(out[name].dtype))
    for name, factor in factors.items():
        out[name] = (out[name] * factor).astype(out[name].dtype)
    return out
```

```python
from contextlib import ExitStack

import concourse.bass as bass
from concourse import mybir

F32 = mybir.dt.float32
F32R = mybir.dt.float32r
F16 = mybir.dt.float16
I32 = mybir.dt.int32
ALU = mybir.AluOpType
ACT = mybir.ActivationFunctionType
AX = mybir.AxisListType.X

P = 128
N = 1250
D = 512
E = 20000
LAYERS = 3
NT = -(-N // P)
NP = NT * P
DC = D // P
NG = 3
G = 418
NGP = NG * G
TAIL = N - (NT - 1) * P
LASTG = N - (NG - 1) * G

HALF = NP // 2
HB = HALF // 2
SUB = P // 2
STEPS = NP // SUB
WIN = 10
CHUNKS = 160
WINDOWS = CHUNKS // WIN
EP = CHUNKS * P
NO_NODE = 4096
ROWS = 125
ROWLEN = E // ROWS

SPL = 8
KB = SPL + 1
BLK = DC * D
INV_STEP = 2.5
LEAK = 0.2
EPS = 1e-5
PAIR = 2
UNITS = KB * DC // PAIR
SUNITS = SPL * DC // PAIR
RING = 6
AHEAD = 4
YB = 4


def build(nc, x, xT, src_c, dst_c, dst_flat, W, a, wk, gwT, gvec, outT):
    x1_dram = nc.dram_tensor("x1_scratch", (D, N), F32, kind="Internal").ap()

    with ExitStack() as ctx:
        def sem(name):
            return ctx.enter_context(nc.semaphore(name))

        base = 16512
        used = {}

        def at(name, col, shape, dt):
            size = 1
            for s in shape:
                size *= s
            size = size * (2 if dt == F16 else 4)
            used[name] = (col, col + -(-size // 4))
            return nc.alloc_sbuf_tensor_at(name, [P, *shape], dt, offset=base + 4 * col)

        Z1, Z2, Z3, Z4, Z5 = 0, 12800, 31232, 36352, 50432
        CT = at("CT", Z1, [NT, NP], F16)
        C16 = at("C16", Z1 + 6400, [NT, NP], F16)
        Wat = at("Wat", Z1, [DC, D], F32)
        abc = at("abc", Z1 + 2048, [2, D], F32)
        XT = at("XT", Z1, [DC, NGP], F32)
        CF = at("CF", Z1, [NT, NP], F32R)
        WKf = at("WKf", Z2, [KB, BLK], F32)
        WKh = at("WKh", Z2, [KB, 2, BLK], F16)
        XH = at("XH", Z2, [DC, NP], F32R)
        XL = at("XL", Z2 + 5120, [DC, NP], F32R)
        GWf = at("GWf", Z2 + 10240, [DC, D], F32)
        GWH = at("GWH", Z2 + 12288, [DC, D], F32R)
        GWL = at("GWL", Z2 + 14336, [DC, D], F32R)
        C9 = at("C9", Z2 + 16384, [NP], F16)
        XR = at("XR", Z2, [DC, NGP], F32)
        hx = at("hx", Z3, [NT, D], F32)
        EX = at("EX", Z3, [4, NP], F32)
        AGG = at("AGG", Z3, [DC, NGP], F32)
        Z = at("Z", Z3, [DC, NGP], F32)
        hH = at("hH", Z4, [NT, D], F16)
        hL = at("hL", Z4 + 2560, [NT, D], F16)
        OS = at("OS", Z4 + 5120, [2, WIN, HALF], F16)
        AL = at("AL", Z4 + 5120, [NT, NP], F16)
        U = at("U", Z4 + 5120, [NP], F32)
        SCR = at("SCR", Z4 + 6400, [NP], F32)
        MSK = at("MSK", Z4 + 7680, [2, NP], F16)
        DG = at("DG", Z4 + 8960, [2, NT, P], F32)
        OD = at("OD", Z4 + 11520, [2, P, WIN], F16)
        WAB = at("WAB", Z4 + 12800, [2, D], F32)
        PQ = at("PQ", Z4 + 11520, [2, NP], F32)
        WS = at("WS", Z4 + 11520, [2, BLK // 2], F32)
        UC = PAIR * G
        kv, ka, kb, kc01, kd = (at(f"k{n}", Z4 + i * 2 * UC, [2, UC], F32) for i, n in enumerate("vabcd"))
        kc2 = at("kc2", Z1 + DC * NGP, [UC], F32)
        kc = [kc01[:, 0, :], kc01[:, 1, :], kc2[:, :]]
        BHL = at("BHL", Z4 + 10 * UC, [RING, 2, PAIR, G], F16)
        sq2 = at("sq2", Z4, [2, DC, G], F32)
        rst = at("rst", Z4 + 2 * DC * G, [2, G], F32)
        YH = at("YH", Z4, [NT, D], F32R)
        YL = at("YL", Z4 + 5120, [NT, D], F32R)
        ZT = at("ZT", Z4 + 10240, [2, NGP], F32)
        z5 = [Z5]

        def small(name, shape, dt=F32):
            h = at(name, z5[0], shape, dt)
            z5[0] = -(-used[name][1] // 8) * 8
            return h

        ident = small("ident", [P])
        ones = small("ones", [P])
        ident16 = small("ident16", [P], F16)
        ones16 = small("ones16", [P], F16)
        iota = small("iota", [HALF], F16)
        key = small("key", [CHUNKS])
        srcm = small("srcm", [CHUNKS])
        kwin = small("kwin", [2, WIN], F16)
        swin = small("swin", [2, WIN])
        koff = small("koff", [STEPS + 1])
        cnt = small("cnt", [STEPS + 2])
        ctl = small("ctl", [STEPS + 4], I32)
        wacol = small("wacol", [2 * DC])
        cen = small("cen", [SPL])
        tiny = small("tiny", [2])
        mv = small("mv", [3, NT])
        lnr = small("lnr", [2, NT])
        st = small("st", [2, NT])
        mx = small("mx", [6, NT])
        tmin = small("tmin", [2])
        wss = small("wss", [KB])
        wsc = small("wsc", [4])
        dvc = small("dvc", [NT])
        gpar = small("gpar", [3, LAYERS, DC])
        bnz = small("bnz", [NG, 6])
        bnm = small("bnm", [2])
        bnc = small("bnc", [4, DC])
        dvb_at = z5[0]
        dvb = small("dvb", [NP])
        assert base + 4 * z5[0] <= 229344, z5[0]
        dsti = at("dsti", dvb_at, [CHUNKS], I32)
        srci = at("srci", dvb_at + 160, [CHUNKS], I32)
        rowi = at("rowi", dvb_at + 320, [ROWLEN + 1], I32)
        rowf = at("rowf", dvb_at + 488, [ROWLEN + 1], F32)
        dstf = at("dstf", dvb_at + 656, [CHUNKS], F32)
        tmp = at("tmp", dvb_at + 816, [CHUNKS], F32)
        zero16 = at("zero16", dvb_at + 976, [HB], F16)
        iotaw = at("iotaw", dvb_at, [P, WIN], F16)
        WS3 = at("WS3", dvb_at, [BLK // 2], F32)
        junk = at("junk", Z4 + 13824, [CHUNKS], F32)
        JC = at("JC", Z4 + 5120, [STEPS, CHUNKS], F32)
        JW = at("JW", Z4 + 2560, [2 * DC, D], F16)
        JH = at("JH", Z4 + 5120, [2 * NT, D], F16)
        dsti2 = at("dsti2", Z4, [CHUNKS], I32)
        rowd = at("rowd", Z4 + 160, [ROWLEN], F32)
        DVD = at("DVD", Z4 + 5120, [NT, P], F32)
        tot = at("tot", Z4 + 320, [4, STEPS + 2], F32)
        RDN = at("RDN", Z4 + 13568, [G], F32)

        bank = ctx.enter_context(nc.psum_tensor("bank", [P, 8, 512], F32))
        WSR = [WS[:, 0, :], WS[:, 1, :], WS3[:, :]]
        EX2 = [bank[:, 5:8, :].rearrange("p b c -> p (b c)")[:, 0:NP], dvb[:, :]]
        bank16 = bank[:, :, :].rearrange("p b c -> p (b c)").bitcast(F16).rearrange("p (b c) -> p b c", b=8)

        pads_set = sem("pads_set")
        consts_set = sem("consts_set")
        consts2_set = sem("consts2_set")
        edges_in = sem("edges_in")
        x_in = sem("x_in")
        att_in = sem("att_in")
        wk_in = sem("wk_in")
        xT_in = sem("xT_in")
        gw_in = sem("gw_in")
        gpar_in = sem("gpar_in")
        counts_done = sem("counts_done")
        totals_done = sem("totals_done")
        ctl_set = sem("ctl_set")
        iota_wide = sem("iota_wide")
        window_set = sem("window_set")
        g_window_set = sem("g_window_set")
        onehots = sem("onehots")
        g_onehots = sem("g_onehots")
        g_onehots_used = sem("g_onehots_used")
        sub_counted = sem("sub_counted")
        sub_copied = sem("sub_copied")
        tposed = sem("tposed")
        tposed_out = sem("tposed_out")
        squares = sem("squares")
        degs_done = sem("degs_done")
        degs_out = sem("degs_out")
        ln_rowstd = sem("ln_rowstd")
        dv_diag = sem("dv_diag")
        dv_spread = sem("dv_spread")
        norm_set = sem("norm_set")
        ln_std = sem("ln_std")
        bn_var = sem("bn_var")
        bn_std = sem("bn_std")
        wa_diag = sem("wa_diag")
        wa_spread = sem("wa_spread")
        wa_set = sem("wa_set")
        ln_rows = sem("ln_rows")
        h_rows = sem("h_rows")
        h_high = sem("h_high")
        h_low = sem("h_low")
        t_diag = sem("t_diag")
        t_spread = sem("t_spread")
        t_used = sem("t_used")
        pq_diag = sem("pq_diag")
        pq_spread = sem("pq_spread")
        pq_set = sem("pq_set")
        exps = sem("exps")
        att_f32 = sem("att_f32")
        att_high = sem("att_high")
        att_low = sem("att_low")
        agg_unit = sem("agg_unit")
        agg_out = sem("agg_out")
        rden_set = sem("rden_set")
        xpad_set = sem("xpad_set")
        sumsq_set = sem("sumsq_set")
        sumsq_done = sem("sumsq_done")
        wscale_set = sem("wscale_set")
        wk_scaled = sem("wk_scaled")
        wk_high = sem("wk_high")
        wk_low = sem("wk_low")
        k_abs = sem("k_abs")
        k_clip = sem("k_clip")
        k_sq = sem("k_sq")
        k_cubea = sem("k_cubea")
        k_cubeb = sem("k_cubeb")
        k_val = sem("k_val")
        k_silu = sem("k_silu")
        k_high = sem("k_high")
        k_low = sem("k_low")
        k_used = sem("k_used")
        kan_copied = sem("kan_copied")
        x1_out = sem("x1_out")
        ln_sum = sem("ln_sum")
        ln_dev = sem("ln_dev")
        ln_sqr = sem("ln_sqr")
        ln_var = sem("ln_var")
        ln_y = sem("ln_y")
        x_high = sem("x_high")
        x_low = sem("x_low")
        c9_set = sem("c9_set")
        cf_copied = sem("cf_copied")
        cf_set = sem("cf_set")
        xpads_zero = sem("xpads_zero")
        gw_high = sem("gw_high")
        gw_low = sem("gw_low")
        y_done = sem("y_done")
        y_high = sem("y_high")
        y_low = sem("y_low")
        z_done = sem("z_done")
        z_out = sem("z_out")
        bn_set = sem("bn_set")
        relu_set = sem("relu_set")
        xr_in = sem("xr_in")
        out_set = sem("out_set")
        stored = sem("stored")

        block = ctx.enter_context(nc.Block())

        @block.sync
        def _(sp):
            sp.dma_start(dsti[:, :], dst_c).then_inc(edges_in, 16)
            sp.dma_start(srci[:, :], src_c).then_inc(edges_in, 16)
            sp.dma_start(rowi[0:ROWS, :], bass.AP(dst_flat.tensor, 0, [[ROWLEN, ROWS], [1, ROWLEN + 1]])
                         ).then_inc(edges_in, 16)
            sp.dma_start(Wat[:, :, :], W.rearrange("(c p) o -> p c o", p=P)).then_inc(att_in, 16)
            sp.dma_start(abc[:, :, :].rearrange("p a b -> p (a b)"), bass.AP(a.tensor, 0, [[0, P], [1, 2 * D]])
                         ).then_inc(att_in, 16)
            sp.wait_ge(pads_set, 1)
            sp.dma_start(hx[:, 0:NT - 1, :], x[0:(NT - 1) * P, :].rearrange("(t p) d -> p t d", p=P)).then_inc(x_in, 16)
            sp.dma_start(hx[0:TAIL, NT - 1, :], x[(NT - 1) * P:N, :]).then_inc(x_in, 16)
            for i in range(KB):
                if i >= 1:
                    sp.wait_ge(wk_in, 16 * i)
                sp.dma_start(WKf[:, i, :].rearrange("p (c o) -> p c o", c=DC),
                             wk[i * D:(i + 1) * D, :].rearrange("(c p) o -> p c o", p=P)).then_inc(wk_in, 16)
            sp.dma_start(gpar[:, :, :, :], gvec).then_inc(gpar_in, 16)
            sp.wait_ge(agg_unit, (DC + 1) * NG)
            sp.dma_start(XT[:, :, 0:N], xT.rearrange("(c p) n -> p c n", p=P)).then_inc(xT_in, 16)
            sp.wait_ge(kan_copied, NG + 1)
            sp.dma_start(x1_dram.rearrange("(c p) n -> p c n", p=P), XT[:, :, 0:N]).then_inc(x1_out, 16)
            for l in range(LAYERS):
                if l > 0:
                    sp.wait_ge(gw_low, l)
                else:
                    sp.wait_ge(k_used, NG * UNITS + RING)
                sp.dma_start(GWf[:, :, :], gwT[l].rearrange("(c p) o -> p c o", p=P)).then_inc(gw_in, 16)
            sp.wait_ge(y_done, LAYERS * NT)
            sp.wait_ge(x1_out, 16)
            sp.dma_start(XR[:, :, 0:N], x1_dram.rearrange("(c p) n -> p c n", p=P)).then_inc(xr_in, 16)
            for c in range(DC):
                sp.wait_ge(out_set, c + 1)
                sp.dma_start(outT[c * P:(c + 1) * P, :], Z[:, c, 0:N]).then_inc(stored, 16)
            sp.wait_ge(stored, 16 * DC)

        @block.gpsimd
        def _(pool):
            nc.gpsimd.memset(hx[:, NT - 1, :], 0.0).then_inc(pads_set, 1)
            nc.gpsimd.iota(iota[:, :], pattern=[[1, HALF]], base=0, channel_multiplier=0,
                           allow_small_or_imprecise_dtypes=True).then_inc(consts_set, 1)
            nc.gpsimd.memset(ident[:, :], 0.0)
            pool.drain()
            nc.gpsimd.affine_select(out=ident[:, :], in_=ident[:, :], compare_op=ALU.not_equal, fill=1.0, base=0,
                                    pattern=[[-1, P]], channel_multiplier=1)
            pool.drain()
            nc.gpsimd.tensor_copy(ident16[:, :], ident[:, :]).then_inc(consts_set, 1)
            for t in range(NT):
                pool.wait_ge(h_high, t + 1)
                nc.gpsimd.tensor_tensor(hL[:, t, :], hx[:, t, :], hH[:, t, :], ALU.subtract).then_inc(h_low, 1)
            for j in range(NT):
                pool.wait_ge(att_high, j + 1)
                nc.gpsimd.tensor_tensor(AL[:, j, :], EX[:, j % 4, :], CT[:, j, :], ALU.subtract).then_inc(att_low, 1)
            for n in range(2 * KB):
                pool.wait_ge(wk_scaled, 2 * (n // 2) + 2)
                pool.wait_ge(wk_high, n + 1)
                part = slice(n % 2 * (BLK // 2), (n % 2 + 1) * (BLK // 2))
                nc.gpsimd.tensor_tensor(WKh[:, n // 2, 1, part], WSR[n % 3], WKh[:, n // 2, 0, part], ALU.subtract
                                        ).then_inc(wk_low, 1)
            pool.wait_ge(agg_unit, (DC + 1) * NG)
            nc.gpsimd.memset(XT[:, :, N:NGP], 0.0).then_inc(xpad_set, 1)
            with pool.Fori(0, NG) as g:
                for u in range(SUNITS):
                    pool.wait_ge(k_sq, g * SUNITS + (u + 1))
                    nc.gpsimd.tensor_tensor(kd[:, u % 2, :], kd[:, u % 2, :], kb[:, u % 2, :], ALU.mult
                                            ).then_inc(k_cubeb, 1)
            pool.wait_ge(k_used, NG * UNITS + RING)
            nc.gpsimd.memset(XH[:, :, NGP:NP].bitcast(F32), 0.0).then_inc(xpads_zero, 1)
            nc.gpsimd.memset(XL[:, :, NGP:NP].bitcast(F32), 0.0).then_inc(xpads_zero, 1)

            def split_weights(l):
                pool.wait_ge(gw_high, l + 1)
                nc.gpsimd.tensor_tensor(GWL[:, :, :], GWf[:, :, :], GWH[:, :, :].bitcast(F32), ALU.subtract
                                        ).then_inc(gw_low, 1)

            split_weights(0)
            for t in range(NT):
                pool.wait_ge(cf_copied, t + 1)
                d = CF[:, t, t * P:(t + 1) * P]
                nc.gpsimd.tensor_tensor(d, d.bitcast(F32), ident[:, :], ALU.add).then_inc(cf_set, 1)
            for l in range(1, LAYERS):
                pool.wait_ge(y_done, NT * l)
                split_weights(l)

        @block.scalar
        def _(act):
            act.wait_ge(wa_spread, 1)
            nc.scalar.copy(WAB[:, :, :], bank[:, 4:6, :]).then_inc(wa_set, 1)
            def copy_sub(t, half, n):
                act.wait_ge(sub_counted, n + 2)
                for s in range(2):
                    src = bank[s * SUB:(s + 1) * SUB, 2 * half:2 * half + 2, 0:HB]
                    dst = CT[half * SUB:(half + 1) * SUB, t:t + 1, s * HALF:(s + 1) * HALF]
                    ins = nc.scalar.copy(dst.rearrange("p a (b c) -> p (a b) c", b=2), src)
                ins.then_inc(sub_copied, 1)

            def statistics(t):
                act.wait_ge(x_in, 32)
                act.wait_ge(wa_set, 1)
                for i in range(2):
                    nc.scalar.activation(bank[:, 4 + i, :], hx[:, t + i, :], ACT.Identity, accum_out=mv[:, 0, t + i:t + i + 1])
                act.drain()
                nc.scalar.mul(mv[:, 1, t:t + 2], mv[:, 0, t:t + 2], -1.0 / D)
                act.drain()
                for i in range(2):
                    nc.scalar.activation(bank[:, 4 + i, :], hx[:, t + i, :], ACT.Square, bias=mv[:, 1, t + i:t + i + 1],
                                         accum_out=mv[:, 2, t + i:t + i + 1])
                act.drain()

            def activations(t):
                act.wait_ge(ln_rows, 1)
                for i in (t, t + 1):
                    nc.scalar.activation(hx[:, i, :], hx[:, i, :], ACT.Relu, bias=lnr[:, 1, i:i + 1],
                                         scale=lnr[:, 0, i:i + 1]).then_inc(h_rows, 1)
                for i in (t, t + 1):
                    act.wait_ge(h_rows, i + 1)
                    nc.scalar.copy(hH[:, i, :], hx[:, i, :]).then_inc(h_high, 1)

            for t in range(NT):
                if t < NT // 2:
                    statistics(2 * t)
                else:
                    activations(2 * t - NT)
                for half in range(2):
                    copy_sub(t, half, 2 * t + (half + 1))
                if t == NT // 2 - 1:
                    nc.scalar.activation(lnr[:, 0, :], mv[:, 2, :], ACT.Sqrt, bias=tiny[:, 1:2], scale=1.0 / D
                                         ).then_inc(ln_rowstd, 1)
                if t < KB:
                    act.wait_ge(wk_in, 16 * (t + 1))
                    nc.scalar.activation(bank[:, 4:8, :].rearrange("p b c -> p (b c)"), WKf[:, t, :], ACT.Square,
                                         accum_out=wss[:, t:t + 1]).then_inc(squares, 1)
                    act.wait_ge(squares, t + 1)
            for t in range(NT):
                for b in range(2):
                    act.wait_ge(tposed, 2 * t + b + 1)
                    nc.scalar.copy(C16[:, 5 * b:5 * b + 5, t * P:(t + 1) * P],
                                   bank16[:, 2 * (t % 2) + b, 0:5 * P].rearrange("p (s c) -> p s c", s=5)
                                   ).then_inc(tposed_out, 1)
            act.wait_ge(degs_done, 1)
            nc.scalar.activation(dvc[:, :], bank[:, 0, 0:NT], ACT.Sqrt, bias=1.0).then_inc(degs_out, 1)
            act.wait_ge(sumsq_done, 1)
            nc.scalar.activation(wsc[:, 2:3], bank[:, 7, 0:1], ACT.Sqrt, bias=tiny[:, 0:1]).then_inc(norm_set, 1)
            act.wait_ge(pq_spread, 1)
            nc.scalar.copy(PQ[:, 0, :], bank[:, 0:3, :].rearrange("p b c -> p (b c)")[:, 0:NP])
            nc.scalar.copy(PQ[:, 1, :], bank[:, 3:6, :].rearrange("p b c -> p (b c)")[:, 0:NP]).then_inc(pq_set, 1)
            act.wait_ge(pq_set, 1)
            act.wait_ge(h_low, NT)

            def exponentials(j):
                if j >= 4:
                    act.wait_ge(att_low, j - 3)
                if j >= 2:
                    act.wait_ge(att_f32, j - 1)
                nc.scalar.activation(EX[:, j % 4, :], PQ[:, 0, :], ACT.Exp, bias=mx[:, 4, j:j + 1])
                nc.scalar.activation(EX2[j % 2], PQ[:, 1, :], ACT.Exp, bias=mx[:, 5, j:j + 1]).then_inc(exps, 1)

            exponentials(0)
            for j in range(NT):
                if j + 1 < NT:
                    exponentials(j + 1)
                act.wait_ge(att_f32, j + 1)
                nc.scalar.copy(CT[:, j, :], EX[:, j % 4, :]).then_inc(att_high, 1)
            act.wait_ge(wscale_set, 1)
            act.wait_ge(att_f32, NT)
            for i in range(KB):
                for n in (2 * i, 2 * i + 1):
                    if n >= 3:
                        act.wait_ge(wk_low, n - 2)
                    part = slice(n % 2 * (BLK // 2), (n % 2 + 1) * (BLK // 2))
                    nc.scalar.mul(WSR[n % 3], WKf[:, i, part], wsc[:, 0:1]).then_inc(wk_scaled, 1)
                for n in (2 * i, 2 * i + 1):
                    act.wait_ge(wk_scaled, n + 1)
                    part = slice(n % 2 * (BLK // 2), (n % 2 + 1) * (BLK // 2))
                    nc.scalar.copy(WKh[:, i, 0, part], WSR[n % 3]).then_inc(wk_high, 1)

            act.wait_ge(agg_out, NG * DC)
            with act.Fori(0, NG) as g:
                def distance(u):
                    act.wait_ge(agg_out, NG * DC)
                    src = AGG[:, PAIR * (u % 2):PAIR * (u % 2) + PAIR, bass.ds(g * G, G)]
                    nc.scalar.activation(kv[:, u % 2, :].rearrange("p (c n) -> p c n", c=PAIR), src, ACT.Abs,
                                         bias=cen[:, u // 2:u // 2 + 1], scale=INV_STEP).then_inc(k_abs, 1)

                def high(u):
                    act.wait_ge(k_used, g * UNITS + (u + 1))
                    nc.scalar.copy(BHL[:, u % RING, 0, :, :], kc[u % 3].rearrange("p (c n) -> p c n", c=PAIR)
                                   ).then_inc(k_high, 1)

                distance(0)
                for u in range(SUNITS):
                    if u + 1 < SUNITS:
                        distance(u + 1)
                    if u >= 2:
                        act.wait_ge(k_val, g * SUNITS + (u - 1))
                        high(u - 2)
                    act.wait_ge(k_clip, g * SUNITS + (u + 1))
                    act.wait_ge(k_low, g * UNITS + (u + 1))
                    nc.scalar.activation(kc[u % 3], ka[:, u % 2, :], ACT.Square, scale=(1.0 / 6.0) ** 0.5)
                    nc.scalar.activation(kd[:, u % 2, :], kb[:, u % 2, :], ACT.Square, scale=(4.0 / 6.0) ** 0.5
                                         ).then_inc(k_sq, 1)
                for u in range(SUNITS, UNITS):
                    act.wait_ge(k_low, g * UNITS + (u + 1))
                    act.wait_ge(k_val, g * SUNITS + (u - 1))
                    high(u - 2)
                    src = AGG[:, PAIR * (u % 2):PAIR * (u % 2) + PAIR, bass.ds(g * G, G)]
                    nc.scalar.activation(kc[u % 3].rearrange("p (c n) -> p c n", c=PAIR), src, ACT.Silu
                                         ).then_inc(k_silu, 1)
                for u in range(SUNITS, UNITS):
                    act.wait_ge(k_silu, g * (UNITS - SUNITS) + (u - SUNITS + 1))
                    high(u)
            def deviation(g):
                act.wait_ge(ln_var, g + 1)
                if g >= 2:
                    act.wait_ge(ln_y, g - 1)
                nc.scalar.activation(rst[:, g % 2, :], bank[:, 6 + g % 2, 0:G], ACT.Sqrt, bias=tiny[:, 1:2],
                                     scale=1.0 / D).then_inc(ln_std, 1)

            def high_part(g):
                act.wait_ge(ln_y, g + 1)
                nc.scalar.activation(XH[:, :, g * G:(g + 1) * G], AGG[:, :, g * G:(g + 1) * G], ACT.Relu
                                     ).then_inc(x_high, 1)

            for g in range(NG):
                act.wait_ge(ln_dev, g + 1)
                if g >= 2:
                    act.wait_ge(ln_var, g - 1)
                nc.scalar.activation(sq2[:, g % 2, :, :], AGG[:, :, g * G:(g + 1) * G], ACT.Square).then_inc(ln_sqr, 1)
                if g == 0:
                    nc.scalar.copy(C9[:, :], C16[:, NT - 1, :]).then_inc(c9_set, 1)
                if g == 1:
                    act.wait_ge(gw_in, 16)
                    nc.scalar.copy(GWH[:, :, :], GWf[:, :, :]).then_inc(gw_high, 1)
                if g >= 1:
                    deviation(g - 1)
                    high_part(g - 1)
            deviation(NG - 1)
            high_part(NG - 1)

            def widen(t):
                act.wait_ge(c9_set, 1)
                act.wait_ge(x1_out, 16)
                act.wait_ge(ln_dev, NG)
                if t >= NT // 2:
                    act.wait_ge(cf_copied, t)
                src = C9[:, :] if t == NT - 1 else C16[:, t, :]
                nc.scalar.copy(CF[:, t, :], src).then_inc(cf_copied, 1)

            def layer(l, first, last):
                for t in range(NT):
                    if first:
                        widen(t)
                    act.wait_ge(y_done, l * NT + (t + 1))
                    nc.scalar.mul(YH[:, t, :], bank[:, t % YB, :], dvc[:, t:t + 1]).then_inc(y_high, 1)
                if not last:
                    act.wait_ge(gw_in, l * 16 + 32)
                    nc.scalar.copy(GWH[:, :, :], GWf[:, :, :]).then_inc(gw_high, 1)
                for c in range(DC):
                    act.wait_ge(bn_var, l * DC + (c + 1))
                    nc.scalar.activation(bnc[:, 2, c:c + 1], bnm[:, 1:2], ACT.Sqrt, bias=tiny[:, 1:2]).then_inc(bn_std, 1)
                    act.wait_ge(bn_set, l * DC + (c + 1))
                    nc.scalar.activation(Z[:, c, :], Z[:, c, :], ACT.Relu, bias=bnc[:, 1, c:c + 1],
                                         scale=bnc[:, 0, c:c + 1]).then_inc(relu_set, 1)
                    if not last:
                        act.wait_ge(relu_set, l * DC + (c + 1))
                        nc.scalar.copy(XH[:, c, 0:NGP], Z[:, c, :]).then_inc(x_high, 1)

            layer(0, True, False)
            with act.Fori(1, LAYERS - 1) as l:
                layer(l, False, False)
            layer(LAYERS - 1, False, True)

        @block.vector
        def _(dve):
            V = nc.vector

            def each(ap, n):
                return bass.AP(ap.tensor, ap.offset, [ap.ap[0], [0, n], ap.ap[1]])

            def wide(ap, m):
                return bass.AP(ap.tensor, ap.offset, [ap.ap[0], ap.ap[1], [0, m]])

            def diagonals(out, cols, done):
                n = out.shape[1]
                V.tensor_tensor(out, each(ident[:, :], n), wide(cols, P), ALU.mult).then_inc(done, 1)

            V.memset(ones[:, :], 1.0)
            V.memset(ones16[:, :], 1.0)
            V.memset(zero16[:, :], 0.0)
            V.memset(cnt[:, :], 0.0)
            for p in range(SPL):
                V.memset(cen[:, p:p + 1], 0.5 * SPL - 0.5 - p)
            V.memset(tiny[:, 0:1], 1e-30)
            V.memset(tiny[:, 1:2], EPS)
            dve.drain()
            V.memset(wsc[:, :], 0.0).then_inc(consts2_set, 1)
            for i, (free, n) in enumerate(((sub_counted, 2), (g_onehots_used, 2), (sub_copied, 2), (k_used, RING),
                                           (k_low, 3), (kan_copied, 1), (y_low, YB), (z_out, YB))):
                V.memset(junk[:, i:i + 1], 0.0).then_inc(free, n)
            dve.wait_ge(edges_in, 48)
            V.tensor_copy(dstf[:, :], dsti[:, :])
            V.tensor_copy(srcm[:, :], srci[:, :])
            V.tensor_scalar(dsti2[:, :], dsti[:, :], 6, 6, ALU.arith_shift_right, ALU.arith_shift_left)
            V.tensor_copy(rowf[0:ROWS, :], rowi[0:ROWS, :])
            dve.drain()
            V.tensor_scalar(tmp[:, :], srcm[:, :], float(HALF), None, ALU.is_ge)
            V.tensor_copy(key[:, :], dsti2[:, :])
            V.tensor_tensor(rowd[0:ROWS, :], rowf[0:ROWS, 1:ROWLEN + 1], rowf[0:ROWS, 0:ROWLEN], ALU.subtract)
            dve.drain()
            V.tensor_tensor(key[:, :], key[:, :], dstf[:, :], ALU.add)
            V.scalar_tensor_tensor(srcm[:, :], tmp[:, :], -float(HALF), srcm[:, :], ALU.mult, ALU.add)
            V.tensor_scalar(junk[0:ROWS, :], rowd[0:ROWS, :], 0.0, None, ALU.is_lt, ALU.add,
                            accum_out=cnt[0:ROWS, STEPS + 1:STEPS + 2])
            dve.drain()
            V.scalar_tensor_tensor(key[:, :], tmp[:, :], float(SUB), key[:, :], ALU.mult, ALU.add)
            for d in range(1, STEPS + 1):
                ins = V.tensor_scalar(JC[:, d - 1, :], dstf[:, :], float(SUB * d), None, ALU.is_lt, ALU.add,
                                      accum_out=cnt[:, d:d + 1])
            ins.then_inc(counts_done, 1)
            dve.wait_ge(att_in, 32)
            for k in range(2):
                for c in range(DC):
                    V.tensor_tensor_reduce(out=JW[:, k * DC + c, :], in0=Wat[:, c, :], in1=abc[:, k, :], scale=1.0, scalar=0.0,
                                           op0=ALU.mult, op1=ALU.add, accum_out=wacol[:, k * DC + c:k * DC + c + 1])
            dve.drain()
            dve.wait_ge(consts_set, 2)
            diagonals(DG[:, 0, 0:2 * DC, :], wacol[:, :], wa_diag)
            dve.wait_ge(totals_done, 1)
            V.tensor_copy(tot[0:1, 0, :], bank[0:1, 0, 0:STEPS + 2])
            V.tensor_copy(ctl[0:1, 0:STEPS], bank[0:1, 0, 0:STEPS])
            dve.drain()
            V.tensor_scalar(ctl[0:1, 0:STEPS], ctl[0:1, 0:STEPS], 7, None, ALU.arith_shift_right)
            dve.drain()
            V.tensor_scalar(ctl[0:1, 0:STEPS], ctl[0:1, 0:STEPS], CHUNKS - WIN, None, ALU.min)
            dve.drain()
            V.tensor_copy(tot[0:1, 1, 0:STEPS], ctl[0:1, 0:STEPS])
            dve.drain()
            V.scalar_tensor_tensor(tot[0:1, 2, 0:STEPS], tot[0:1, 1, 0:STEPS], -float(P), tot[0:1, 0, 1:STEPS + 1],
                                   ALU.mult, ALU.add)
            dve.drain()
            V.tensor_scalar(tot[0:1, 2, 0:STEPS], tot[0:1, 2, 0:STEPS], float(WIN * P), 0.0, ALU.subtract, ALU.max)
            dve.drain()
            V.tensor_copy(tot[0:1, 2, STEPS:STEPS + 1], tot[0:1, 0, STEPS + 1:STEPS + 2])
            dve.drain()
            V.tensor_reduce(tot[0:1, 3, 0:1], tot[0:1, 2, 0:STEPS + 1], AX, ALU.add)
            dve.drain()
            V.tensor_copy(ctl[0:1, STEPS:STEPS + 1], tot[0:1, 3, 0:1]).then_inc(ctl_set, 1)
            dve.wait_ge(ctl_set, 1)
            dve.wait_ge(wa_spread, 1)

            V.tensor_scalar(koff[:, :], iota[:, 0:STEPS + 1], float(P), None, ALU.mult)
            V.tensor_copy(iotaw[:, :, :], wide(iota[:, 0:P], WIN)).then_inc(iota_wide, 1)
            dve.wait_ge(iota_wide, 1)

            def extract(first, step, buf, done):
                V.tensor_scalar(kwin[:, buf, :], key[:, bass.ds(first, WIN)], koff[:, bass.ds(step, 1)], None,
                                ALU.subtract)
                V.tensor_copy(swin[:, buf, :], srcm[:, bass.ds(first, WIN)]).then_inc(done, 1)

            def destination_rows(buf):
                V.tensor_tensor(OD[:, buf, :, :], iotaw[:, :, :], each(kwin[:, buf, :], P), ALU.is_equal)

            def source_rows(buf, k0, k1, ready):
                for k in range(k0, k1):
                    ins = V.tensor_scalar(OS[:, buf, k, :], iota[:, :], swin[:, buf, k:k + 1], None, ALU.is_equal)
                ins.then_inc(ready, 1)

            def row_scales():
                dve.wait_ge(ln_rowstd, 1)
                V.reciprocal(lnr[:, 0, :], lnr[:, 0, :])
                dve.drain()
                V.tensor_tensor(lnr[:, 1, :], mv[:, 1, :], lnr[:, 0, :], ALU.mult).then_inc(ln_rows, 1)

            bad = dve.value_load(ctl[0:1, STEPS:STEPS + 1], min_val=0, max_val=1 << 20)
            with dve.If(bad > 0):
                def every_window(d):
                    with dve.Fori(0, WINDOWS // 2) as w:
                        for buf in range(2):
                            n = (d * (WINDOWS // 2) + w) * 2 + buf
                            dve.wait_ge(g_onehots_used, n + 1)
                            extract(w * (2 * WIN) + buf * WIN, d, buf, g_window_set)
                            dve.wait_ge(g_window_set, n + 1)
                            destination_rows(buf)
                            source_rows(buf, 0, WIN // 2, g_onehots)
                            source_rows(buf, WIN // 2, WIN, g_onehots)

                with dve.Fori(0, STEPS // 2) as d:
                    every_window(d)
                row_scales()
                with dve.Fori(STEPS // 2, STEPS) as d:
                    every_window(d)
                dve.nop()
            with dve.Else():
                extract(dve.value_load(ctl[0:1, 0:1], min_val=0, max_val=CHUNKS - WIN), 0, 0, window_set)
                def one_window(t):
                    for half in range(2):
                        dve.wait_ge(sub_counted, t * 2 + (half + 1))
                        dve.wait_ge(window_set, t * 2 + (half + 1))
                        destination_rows(half)
                        source_rows(half, 0, WIN // 2, onehots)
                        first = dve.value_load(ctl[0:1, bass.ds(t * 2 + (half + 1), 1)], min_val=0, max_val=CHUNKS - WIN)
                        dve.drain()
                        extract(first, t * 2 + (half + 1), 1 - half, window_set)
                        source_rows(half, WIN // 2, WIN, onehots)

                with dve.Fori(0, NT // 2) as t:
                    one_window(t)
                row_scales()
                with dve.Fori(NT // 2, NT) as t:
                    one_window(t)
                dve.nop()

            dve.wait_ge(wa_set, 1)
            dve.wait_ge(sub_counted, STEPS + 2)
            for t in range(NT):
                dve.wait_ge(h_rows, t + 1)
                for k in range(2):
                    V.tensor_tensor_reduce(out=JH[:, 2 * t + k, :], in0=hx[:, t, :], in1=WAB[:, k, :], scale=1.0, scalar=0.0,
                                           op0=ALU.mult, op1=ALU.add, accum_out=st[:, k, t:t + 1])
            dve.drain()
            diagonals(DG[:, 0, :, :], st[:, 1, :], t_diag)
            dve.wait_ge(squares, KB)
            V.tensor_reduce(wsc[:, 0:1], wss[:, :], AX, ALU.add).then_inc(sumsq_set, 1)
            V.tensor_copy(mx[:, 4, :], st[:, 1, :])
            V.tensor_scalar(mx[:, 5, :], st[:, 1, :], LEAK, None, ALU.mult)
            dve.wait_ge(t_spread, 1)
            trow = bank[:, 5:8, :].rearrange("p b c -> p (b c)")[:, 0:NP]
            V.tensor_reduce(tmin[:, 0:1], trow, AX, ALU.min)
            dve.drain()
            V.tensor_scalar(tmin[:, 1:2], tmin[:, 0:1], 1.0, None, ALU.subtract)
            dve.drain()
            V.tensor_scalar(U[:, :], trow, tmin[:, 1:2], None, ALU.subtract).then_inc(t_used, 1)
            dve.wait_ge(tposed_out, 2 * NT)
            V.tensor_scalar(MSK[:, 0, :], C16[:, 0, :], 1.0, None, ALU.min)
            for s in range(NT):
                dve.drain()
                if s + 1 < NT:
                    V.tensor_scalar(MSK[:, (s + 1) % 2, :], C16[:, s + 1, :], 1.0, None, ALU.min)
                V.tensor_tensor_reduce(out=SCR[:, :], in0=MSK[:, s % 2, :], in1=U[:, :], scale=1.0, scalar=0.0,
                                       op0=ALU.mult, op1=ALU.max, accum_out=mx[:, 0, s:s + 1])
            dve.drain()
            V.scalar_tensor_tensor(mx[:, 0, :], mx[:, 0, :], tmin[:, 1:2], st[:, 0, :], ALU.add, ALU.add)
            dve.drain()
            V.scalar_tensor_tensor(mx[:, 1, :], mx[:, 0, :], LEAK, mx[:, 0, :], ALU.mult, ALU.max)
            dve.drain()
            V.tensor_tensor(mx[:, 2, :], st[:, 0, :], mx[:, 1, :], ALU.subtract)
            V.scalar_tensor_tensor(mx[:, 3, :], st[:, 0, :], LEAK, mx[:, 1, :], ALU.mult, ALU.subtract)
            dve.drain()
            for k in range(2):
                diagonals(DG[:, k, :, :], mx[:, 2 + k, :], pq_diag)
            dve.wait_ge(norm_set, 1)
            V.reciprocal(wsc[:, 1:2], wsc[:, 2:3])
            dve.drain()
            V.tensor_scalar(wsc[:, 1:2], wsc[:, 1:2], 16384.0, None, ALU.mult)
            dve.drain()
            V.tensor_scalar(wsc[:, 0:1].bitcast(I32), wsc[:, 1:2].bitcast(I32), 0x7F800000, None, ALU.bitwise_and)
            dve.drain()
            V.reciprocal(wsc[:, 1:2], wsc[:, 0:1]).then_inc(wscale_set, 1)
            for j in range(NT):
                dve.wait_ge(exps, j + 1)
                V.tensor_tensor(EX[:, j % 4, :], EX[:, j % 4, :], EX2[j % 2], ALU.max)
                dve.drain()
                V.scalar_tensor_tensor(EX[:, j % 4, :], EX[:, j % 4, :], 1.0, CT[:, j, :], ALU.min, ALU.mult
                                       ).then_inc(att_f32, 1)
            for g in range(NG):
                u = (DC + 1) * g
                dve.wait_ge(agg_unit, u + 1)
                dve.drain()
                V.tensor_scalar(RDN[:, :], bank[:, u % 8, 0:G], 1e-30, None, ALU.max)
                dve.drain()
                V.reciprocal(RDN[:, :], RDN[:, :]).then_inc(rden_set, 1)
                dve.wait_ge(rden_set, g + 1)
                for c in range(DC):
                    dve.wait_ge(agg_unit, u + 2 + c)
                    V.tensor_tensor(AGG[:, c, g * G:(g + 1) * G], bank[:, (u + 1 + c) % 8, 0:G], RDN[:, :], ALU.mult
                                    ).then_inc(agg_out, 1)

            V.reciprocal(dvc[:, :], dvc[:, :])
            dve.drain()
            diagonals(DG[:, 0, :, :], dvc[:, :], dv_diag)
            dve.wait_ge(dv_spread, 1)
            dve.wait_ge(wk_low, 2 * KB)
            V.tensor_copy(dvb[:, :], bank[:, 5:8, :].rearrange("p b c -> p (b c)")[:, 0:NP])
            dve.wait_ge(agg_unit, (DC + 1) * NG)

            def low(g, u):
                dve.wait_ge(k_high, g * UNITS + (u + 1))
                V.tensor_tensor(BHL[:, u % RING, 1, :, :].rearrange("p c n -> p (c n)"), kc[u % 3],
                                BHL[:, u % RING, 0, :, :].rearrange("p c n -> p (c n)"), ALU.subtract).then_inc(k_low, 1)

            def turn(g, u):
                v = (u - 1) % 2
                if u < SUNITS:
                    dve.wait_ge(k_abs, g * SUNITS + (u + 1))
                    V.tensor_scalar(ka[:, u % 2, :], kv[:, u % 2, :], 2.0, 2.0, ALU.min, ALU.subtract)
                    V.tensor_scalar(kb[:, u % 2, :], kv[:, u % 2, :], 1.0, 1.0, ALU.min, ALU.subtract
                                    ).then_inc(k_clip, 1)
                if u >= 1:
                    dve.wait_ge(k_sq, g * SUNITS + u)
                    V.tensor_tensor(kc[(u - 1) % 3], kc[(u - 1) % 3], ka[:, v, :], ALU.mult).then_inc(k_cubea, 1)
                if u >= 2:
                    low(g, u - 2)
                if u >= 1:
                    dve.wait_ge(k_cubea, g * SUNITS + u)
                    dve.wait_ge(k_cubeb, g * SUNITS + u)
                    V.tensor_tensor(kc[(u - 1) % 3], kd[:, v, :], kc[(u - 1) % 3], ALU.subtract).then_inc(k_val, 1)

            def group(g, last):
                for u in range(AHEAD, SUNITS + 1):
                    turn(g, u)
                for u in range(SUNITS - 1, UNITS):
                    low(g, u)
                if not last:
                    for u in range(AHEAD):
                        turn(g + 1, u)
                dve.wait_ge(k_used, g * UNITS + (UNITS + RING))
                dve.wait_ge(xT_in, 16)
                dve.wait_ge(xpad_set, 1)
                for c in range(DC):
                    xc = XT[:, c, bass.ds(g * G, G)]
                    ins = V.scalar_tensor_tensor(xc, bank[:, c, 0:G], wsc[:, 1:2], xc, ALU.mult, ALU.add)
                ins.then_inc(kan_copied, 1)

            for u in range(AHEAD):
                turn(0, u)
            with dve.Fori(0, NG - 1) as g:
                group(g, False)
            group(NG - 1, True)

            def centered(g):
                dve.wait_ge(ln_sum, g + 1)
                for c in range(DC):
                    ins = V.scalar_tensor_tensor(AGG[:, c, g * G:(g + 1) * G], bank[:, 4 + g % 2, 0:G], -1.0 / D,
                                                 XT[:, c, g * G:(g + 1) * G], ALU.mult, ALU.add)
                ins.then_inc(ln_dev, 1)

            def normalized(g):
                dve.wait_ge(ln_std, g + 1)
                V.reciprocal(rst[:, g % 2, :], rst[:, g % 2, :])
                dve.drain()
                for c in range(DC):
                    y = AGG[:, c, g * G:(g + 1) * G]
                    ins = V.tensor_tensor(y, y, rst[:, g % 2, :], ALU.mult)
                ins.then_inc(ln_y, 1)

            def split_low(g):
                dve.wait_ge(x_high, g + 1)
                y = slice(g * G, (g + 1) * G)
                V.scalar_tensor_tensor(XL[:, :, y], AGG[:, :, y], 0.0, XH[:, :, y].bitcast(F32), ALU.max, ALU.subtract
                                       ).then_inc(x_low, 1)

            centered(0)
            centered(1)
            for g in range(NG):
                if g >= 1 and g + 1 < NG:
                    centered(g + 1)
                normalized(g)
                split_low(g)

            dve.wait_ge(gpar_in, 16)

            def finish(l, c, last):
                if last:
                    dve.wait_ge(xr_in, 16)
                    dve.wait_ge(relu_set, l * DC + (c + 1))
                    V.tensor_tensor(Z[:, c, 0:N], Z[:, c, 0:N], XR[:, c, 0:N], ALU.add).then_inc(out_set, 1)
                else:
                    dve.wait_ge(x_high, l * DC + (NG + c + 1))
                    V.tensor_tensor(XL[:, c, 0:NGP], Z[:, c, :], XH[:, c, 0:NGP].bitcast(F32), ALU.subtract
                                    ).then_inc(x_low, 1)

            def layer(l, last):
                for t in range(NT):
                    dve.wait_ge(y_high, l * NT + (t + 1))
                    V.scalar_tensor_tensor(YL[:, t, :], bank[:, t % YB, :], dvc[:, t:t + 1], YH[:, t, :].bitcast(F32),
                                           ALU.mult, ALU.subtract).then_inc(y_low, 1)
                for c in range(DC):
                    for g in range(NG):
                        u = c * NG + g
                        dve.wait_ge(z_done, l * (DC * NG) + (u + 1))
                        V.tensor_tensor(Z[:, c, g * G:(g + 1) * G], bank[:, YB + u % YB, 0:G],
                                        dvb[:, g * G:(g + 1) * G], ALU.mult).then_inc(z_out, 1)
                        dve.drain()
                        V.bn_stats(bnz[:, g, :], Z[:, c, g * G:min((g + 1) * G, N)])
                    dve.drain()
                    V.bn_aggr(bnm[:, :], bnz[:, :, :]).then_inc(bn_var, 1)
                    if c >= 1:
                        finish(l, c - 1, last)
                    dve.wait_ge(bn_std, l * DC + (c + 1))
                    b, gamma, beta = (gpar[:, k, bass.ds(l, 1), c] for k in range(3))
                    V.reciprocal(bnc[:, 2, c:c + 1], bnc[:, 2, c:c + 1])
                    V.tensor_tensor(bnc[:, 3, c:c + 1], bnm[:, 0:1], b, ALU.add)
                    dve.drain()
                    V.tensor_tensor(bnc[:, 0, c:c + 1], bnc[:, 2, c:c + 1], gamma, ALU.mult)
                    V.tensor_tensor(bnc[:, 3, c:c + 1], b, bnc[:, 3, c:c + 1], ALU.subtract)
                    dve.drain()
                    V.scalar_tensor_tensor(bnc[:, 1, c:c + 1], bnc[:, 3, c:c + 1], bnc[:, 0, c:c + 1], beta,
                                           ALU.mult, ALU.add).then_inc(bn_set, 1)
                finish(l, DC - 1, last)

            with dve.Fori(0, LAYERS - 1) as l:
                layer(l, False)
            layer(LAYERS - 1, True)

        @block.tensor
        def _(pe):
            mm = nc.tensor.matmul
            pe.wait_ge(consts2_set, 1)
            pe.wait_ge(counts_done, 1)
            mm(bank[0:1, 0, 0:STEPS + 2], ones[:, 0:1], cnt[:, :], start=True, stop=True).then_inc(totals_done, 1)

            def spread(b0, dg, n, done=None):
                for i in range(n):
                    ins = mm(bank[:, b0 + i // 4, (i % 4) * P:(i % 4 + 1) * P], ones[:, :], dg[:, i, :],
                             start=True, stop=True)
                if done is not None:
                    ins.then_inc(done, 1)

            pe.wait_ge(wa_diag, 1)
            spread(4, DG[:, 0, :, :], 2 * DC, wa_spread)
            pe.wait_ge(ctl_set, 1)

            def count(half, buf, n, ready, used, start, stop):
                for k in range(WIN):
                    if k % (WIN // 2) == 0:
                        pe.wait_ge(ready, n * 2 + (k // (WIN // 2) + 1))
                    for b in range(2):
                        ins = mm(bank[:, 2 * half + b, 0:HB], OD[:, buf, :, k], OS[:, buf, k, b * HB:(b + 1) * HB],
                                 start=(start and k == 0), stop=(stop and k == WIN - 1))
                return ins.then_inc(used, 1)

            bad = pe.value_load(ctl[0:1, STEPS:STEPS + 1], min_val=0, max_val=1 << 20)
            with pe.If(bad > 0):
                with pe.Fori(0, NT) as t:
                    for half in range(2):
                        pe.wait_ge(sub_copied, t * 2 + (half + 1))
                        for b in range(2):
                            mm(bank[:, 2 * half + b, 0:HB], ones16[:, :], zero16[:, :], start=True, stop=False)
                        with pe.Fori(0, WINDOWS // 2) as w:
                            for buf in range(2):
                                n = ((t * 2 + half) * (WINDOWS // 2) + w) * 2 + buf
                                count(half, buf, n, g_onehots, g_onehots_used, False, False)
                        for b in range(2):
                            ins = mm(bank[:, 2 * half + b, 0:HB], ones16[:, :], zero16[:, :], start=False, stop=True)
                        ins.then_inc(sub_counted, 1)
                pe.nop()
            with pe.Else():
                with pe.Fori(0, NT) as t:
                    for half in range(2):
                        pe.wait_ge(sub_copied, t * 2 + (half + 1))
                        count(half, half, t * 2 + half, onehots, sub_counted, True, True)
                pe.nop()

            pe.wait_ge(sub_copied, 2 + STEPS)
            for t in range(NT):
                for b in range(2):
                    if t >= 2:
                        pe.wait_ge(tposed_out, 2 * t + b - 3)
                    for s in range(5):
                        ins = nc.tensor.transpose(bank16[:, 2 * (t % 2) + b, s * P:(s + 1) * P],
                                                  CT[:, t, (5 * b + s) * P:(5 * b + s + 1) * P], ident16[:, :])
                    ins.then_inc(tposed, 1)
            pe.wait_ge(tposed_out, 2 * NT)
            for t in range(NT):
                for s in range(NT):
                    ins = mm(bank[:, 0, t:t + 1], C16[:, s, t * P:(t + 1) * P], ones16[:, 0:1], start=(s == 0),
                             stop=(s == NT - 1))
            ins.then_inc(degs_done, 1)
            pe.wait_ge(t_diag, 1)
            pe.wait_ge(squares, KB)
            spread(5, DG[:, 0, :, :], NT, t_spread)
            pe.wait_ge(sumsq_set, 1)
            pe.wait_ge(t_used, 1)
            mm(bank[:, 7, 0:1], ones[:, :], wsc[:, 0:1], start=True, stop=True).then_inc(sumsq_done, 1)
            pe.wait_ge(pq_diag, 2)
            pe.wait_ge(degs_out, 1)
            spread(0, DG[:, 0, :, :], NT)
            spread(3, DG[:, 1, :, :], NT, pq_spread)

            def attend(g, k, j):
                cols = slice(g * G, (g + 1) * G)
                if k == 0:
                    parts = [(ones16[:, :], CT), (ones16[:, :], AL)]
                else:
                    fh, fl = (h[:, j, (k - 1) * P:k * P] for h in (hH, hL))
                    parts = [(fh, CT), (fh, AL), (fl, CT)]
                for i, (lhs, m) in enumerate(parts):
                    ins = mm(bank[:, ((DC + 1) * g + k) % 8, 0:G], lhs, m[:, j, cols],
                             start=(j == 0 and i == 0), stop=(j == NT - 1 and i == len(parts) - 1))
                if j == NT - 1:
                    ins.then_inc(agg_unit, 1)

            pe.wait_ge(h_low, NT)
            pe.wait_ge(pq_set, 1)
            for j in range(NT):
                pe.wait_ge(att_low, j + 1)
                for k in range(DC + 1):
                    attend(0, k, j)
            for g in range(1, NG):
                for k in range(DC + 1):
                    before = (DC + 1) * g + k - 8
                    if before >= 0:
                        pg, pk = divmod(before, DC + 1)
                        if pk == 0:
                            pe.wait_ge(rden_set, pg + 1)
                        else:
                            pe.wait_ge(agg_out, DC * pg + pk)
                    for j in range(NT):
                        attend(g, k, j)

            pe.wait_ge(agg_out, DC * NG)
            pe.wait_ge(dv_diag, 1)
            spread(5, DG[:, 0, :, :], NT, dv_spread)
            pe.wait_ge(wk_low, 2 * KB)
            with pe.Fori(0, NG) as g:
                for u in range(UNITS):
                    pe.wait_ge(k_low, g * UNITS + (u + 4))
                    if u == 0:
                        pe.wait_ge(kan_copied, g + 1)
                    for o in range(DC):
                        for q in range(PAIR):
                            wcol = (PAIR * (u % 2) + q) * D + o * P
                            wh, wl = (WKh[:, u // 2, i, wcol:wcol + P] for i in range(2))
                            bh, bl = (BHL[:, u % RING, i, q, :] for i in range(2))
                            for i, (lhs, rhs) in enumerate(((wh, bh), (wh, bl), (wl, bh))):
                                ins = mm(bank[:, o, 0:G], lhs, rhs, start=(u == 0 and q == 0 and i == 0),
                                         stop=(u == UNITS - 1 and q == PAIR - 1 and i == 2))
                    ins.then_inc(k_used, 1)

            def sums(b, src, done):
                for c in range(DC):
                    ins = mm(bank[:, b, 0:G], ones[:, :], src(c), start=(c == 0), stop=(c == DC - 1))
                ins.then_inc(done, 1)

            def means(g):
                if g >= 2:
                    pe.wait_ge(ln_dev, g - 1)
                sums(4 + g % 2, lambda c: XT[:, c, g * G:(g + 1) * G], ln_sum)

            def variances(g):
                pe.wait_ge(ln_sqr, g + 1)
                if g >= 2:
                    pe.wait_ge(ln_y, g - 1)
                sums(6 + g % 2, lambda c: sq2[:, g % 2, c, :], ln_var)

            pe.wait_ge(kan_copied, NG + 1)
            means(0)
            for g in range(NG):
                if g + 1 < NG:
                    means(g + 1)
                variances(g)

            pe.wait_ge(xpads_zero, 2)

            def feature(t, c):
                xh, xl = (X[:, c, t * P:(t + 1) * P] for X in (XH, XL))
                for i, (lhs, rhs) in enumerate(((xh, GWH), (xh, GWL), (xl, GWH))):
                    ins = mm(bank[:, t % YB, :], lhs, rhs[:, c, :], start=(c == 0 and i == 0),
                             stop=(c == DC - 1 and i == 2))
                if c == DC - 1:
                    ins.then_inc(y_done, 1)

            def layer(l, first):
                pe.wait_ge(gw_low, l + 1)
                if not first:
                    pe.wait_ge(y_low, l * NT + YB)
                    for c in range(DC):
                        pe.wait_ge(x_low, (l - 1) * DC + (NG + c + 1))
                        for t in range(YB):
                            feature(t, c)
                for t in range(0 if first else YB, NT):
                    pe.wait_ge(y_low, l * NT + (t + 1))
                    if first:
                        pe.wait_ge(x_low, min(NG, -(-(t + 1) * P // G)))
                    for c in range(DC):
                        feature(t, c)
                for o in range(DC):
                    for g in range(NG):
                        u = o * NG + g
                        pe.wait_ge(z_out, l * (DC * NG) + (u + 1))
                        for j in range(NT):
                            if u == 0:
                                pe.wait_ge(y_low, l * NT + (YB + j + 1))
                                pe.wait_ge(cf_set, j + 1)
                            for i, Y in enumerate((YH, YL)):
                                ins = mm(bank[:, YB + u % YB, 0:G], Y[:, j, o * P:(o + 1) * P],
                                         CF[:, j, g * G:(g + 1) * G], start=(j == 0 and i == 0),
                                         stop=(j == NT - 1 and i == 1))
                        ins.then_inc(z_done, 1)

            layer(0, True)
            with pe.Fori(1, LAYERS) as l:
                layer(l, False)


_ORDER = ["x", "xT", "src_c", "dst_c", "dst_flat", "W", "a", "wk", "gwT", "gvec"]


def kernel(**inputs):
    import numpy as np
    import concourse.bacc as bacc
    from concourse.bass_utils import run_bass_kernel_spmd

    i = {k: np.asarray(v) for k, v in inputs.items()}
    src = np.pad(i["src"], (0, EP - E))
    dst = np.pad(i["dst"], (0, EP - E), constant_values=NO_NODE)
    arrays = {
        "x": i["x"],
        "xT": i["x"].T,
        "src_c": src.reshape(CHUNKS, P).T,
        "dst_c": dst.reshape(CHUNKS, P).T,
        "dst_flat": dst,
        "W": i["L0_gnn_W"],
        "a": i["L0_gnn_a"].reshape(-1),
        "wk": np.concatenate([i["L0_gnn_spline_w"].transpose(2, 1, 0).reshape(SPL * D, D), i["L0_gnn_base_w"].T]),
        "gwT": i["L1_gnn_W"].transpose(0, 2, 1),
        "gvec": np.stack([i["L1_gnn_b"], i["L1_gnn_gamma"], i["L1_gnn_beta"]]).reshape(3, LAYERS, DC, P
                                                                                     ).transpose(3, 0, 1, 2),
    }
    arrays = {k: np.ascontiguousarray(v) for k, v in arrays.items()}
    nc = bacc.Bacc("TRN2", target_bir_lowering=False, num_devices=1)
    aps = [nc.dram_tensor(f"in_{k}", arrays[k].shape, mybir.dt.from_np(arrays[k].dtype), kind="ExternalInput").ap()
           for k in _ORDER]
    out = nc.dram_tensor("outT", (D, N), F32, kind="ExternalOutput").ap()
    build(nc, *aps, out)
    r = run_bass_kernel_spmd(nc, [{f"in_{k}": v for k, v in arrays.items()}], core_ids=[0])
    return np.ascontiguousarray(r.results[0]["outT"].T)
```

```python
from contextlib import ExitStack

import concourse.bass as bass
from concourse import mybir

F32 = mybir.dt.float32
F32R = mybir.dt.float32r
F16 = mybir.dt.float16
I32 = mybir.dt.int32
ALU = mybir.AluOpType
ACT = mybir.ActivationFunctionType
AX = mybir.AxisListType.X

P = 128
N = 1250
D = 512
E = 20000
LAYERS = 3
NT = -(-N // P)
NP = NT * P
DC = D // P
NG = 3
G = 418
NGP = NG * G
TAIL = N - (NT - 1) * P
LASTG = N - (NG - 1) * G

HALF = NP // 2
HB = HALF // 2
SUB = P // 2
STEPS = NP // SUB
WIN = 10
CHUNKS = 160
WINDOWS = CHUNKS // WIN
EP = CHUNKS * P
NO_NODE = 4096
ROWS = 125
ROWLEN = E // ROWS

SPL = 8
KB = SPL + 1
BLK = DC * D
INV_STEP = 2.5
LEAK = 0.2
EPS = 1e-5
PAIR = 2
UNITS = KB * DC // PAIR
SUNITS = SPL * DC // PAIR
RING = 6
EARLY = 2
AHEAD = 4
YB = 4


def build(nc, x, xT, src_c, dst_c, dst_flat, W, a, wk, gwT, gvec, outT):
    x1_dram = nc.dram_tensor("x1_scratch", (D, N), F32, kind="Internal").ap()

    with ExitStack() as ctx:
        def sem(name):
            return ctx.enter_context(nc.semaphore(name))

        base = 16512
        used = {}

        def at(name, col, shape, dt):
            size = 1
            for s in shape:
                size *= s
            size = size * (2 if dt == F16 else 4)
            used[name] = (col, col + -(-size // 4))
            return nc.alloc_sbuf_tensor_at(name, [P, *shape], dt, offset=base + 4 * col)

        Z1, Z2, Z3, Z4, Z5 = 0, 12800, 31232, 36352, 50432
        CT = at("CT", Z1, [NT, NP], F16)
        C16 = at("C16", Z1 + 6400, [NT, NP], F16)
        Wat = at("Wat", Z1, [DC, D], F32)
        abc = at("abc", Z1 + 2048, [2, D], F32)
        XT = at("XT", Z1, [DC, NGP], F32)
        CF = at("CF", Z1, [NT, NP], F32R)
        WKf = at("WKf", Z2, [KB, BLK], F32)
        WKh = at("WKh", Z2, [KB, 2, BLK], F16)
        XH = at("XH", Z2, [DC, NP], F32R)
        XL = at("XL", Z2 + 5120, [DC, NP], F32R)
        GWf = at("GWf", Z2 + 10240, [DC, D], F32)
        GWH = at("GWH", Z2 + 12288, [DC, D], F32R)
        GWL = at("GWL", Z2 + 14336, [DC, D], F32R)
        C9 = at("C9", Z2 + 16384, [NP], F16)
        XR = at("XR", Z2, [DC, NGP], F32)
        hx = at("hx", Z3, [NT, D], F32)
        EX = at("EX", Z3, [3, NP], F32)
        EX1 = at("EX1", Z3 + 3 * NP, [NP], F32)
        AGG = at("AGG", Z3, [DC, NGP], F32)
        Z = at("Z", Z3, [DC, NGP], F32)
        hH = at("hH", Z4, [NT, D], F16)
        hL = at("hL", Z4 + 2560, [NT, D], F16)
        OS = at("OS", Z4 + 5120, [2, WIN, HALF], F16)
        AL = at("AL", Z4 + 5120, [NT, NP], F16)
        U = at("U", Z4 + 5120, [NP], F32)
        SCR = at("SCR", Z4 + 6400, [NP], F32)
        MSK = at("MSK", Z4 + 7680, [2, NP], F16)
        DG = at("DG", Z4 + 8960, [2, NT, P], F32)
        DG2 = at("DG2", Z4 + 11520, [NT, P], F32)
        OD = at("OD", Z4 + 11520, [2, P, WIN], F16)
        WAB = at("WAB", Z4 + 12800, [2, D], F32)
        PQ = at("PQ", Z4 + 11520, [2, NP], F32)
        WS = at("WS", Z4 + 11520, [2, BLK // 2], F32)
        UC = PAIR * G
        kv, ka, kb, kc01, kd = (at(f"k{n}", Z4 + i * 2 * UC, [2, UC], F32) for i, n in enumerate("vabcd"))
        kc2 = at("kc2", Z1 + DC * NGP, [UC], F32)
        kc = [kc01[:, 0, :], kc01[:, 1, :], kc2[:, :]]
        BHL = at("BHL", Z4 + 10 * UC, [RING, 2, PAIR, G], F16)
        sq2 = at("sq2", Z4, [2, DC, G], F32)
        lnx = at("lnx", Z4 + 2 * DC * G, [2, G], F32)
        lnp = at("lnp", Z4 + 2 * DC * G + 840, [G], F32)
        rst = at("rst", Z4 + 8 * UC, [2, G], F32)
        lnq = at("lnq", Z4 + 8 * UC + 840, [G], F32)
        lnq1 = at("lnq1", Z4 + 13568, [G], F32)
        YH = at("YH", Z4, [NT, D], F32R)
        YL = at("YL", Z4 + 5120, [NT, D], F32R)
        z5 = [Z5]

        def small(name, shape, dt=F32):
            h = at(name, z5[0], shape, dt)
            z5[0] = -(-used[name][1] // 8) * 8
            return h

        ident = small("ident", [P])
        ones = small("ones", [P])
        ident16 = small("ident16", [P], F16)
        ones16 = small("ones16", [P], F16)
        iota = small("iota", [HALF], F16)
        key = small("key", [CHUNKS])
        srcm = small("srcm", [CHUNKS])
        kwin = small("kwin", [2, WIN], F16)
        swin = small("swin", [2, WIN])
        koff = small("koff", [STEPS + 1])
        cnt = small("cnt", [STEPS + 2])
        ctl = small("ctl", [STEPS + 4], I32)
        wacol = small("wacol", [2 * DC])
        cen = small("cen", [SPL])
        tiny = small("tiny", [2])
        mv = small("mv", [3, NT])
        lnr = small("lnr", [2, NT])
        st = small("st", [2, NT])
        mx = small("mx", [6, NT])
        tmin = small("tmin", [2])
        wss = small("wss", [KB])
        wsc = small("wsc", [4])
        dvc = small("dvc", [NT])
        gpar = small("gpar", [3, LAYERS, DC])
        bnz = small("bnz", [NG, 6])
        bnm = small("bnm", [2])
        bnc = small("bnc", [4, DC])
        dvb_at = z5[0]
        dvb = small("dvb", [NP])
        assert base + 4 * z5[0] <= 229344, z5[0]
        dsti = at("dsti", dvb_at, [CHUNKS], I32)
        srci = at("srci", dvb_at + 160, [CHUNKS], I32)
        rowi = at("rowi", dvb_at + 320, [ROWLEN + 1], I32)
        rowf = at("rowf", dvb_at + 488, [ROWLEN + 1], F32)
        dstf = at("dstf", dvb_at + 656, [CHUNKS], F32)
        tmp = at("tmp", dvb_at + 816, [CHUNKS], F32)
        zero16 = at("zero16", dvb_at + 976, [HB], F16)
        iotaw = at("iotaw", dvb_at, [P, WIN], F16)
        WS3 = at("WS3", dvb_at, [BLK // 2], F32)
        junk = at("junk", Z4 + 13824, [CHUNKS], F32)
        JC = at("JC", Z4 + 5120, [STEPS, CHUNKS], F32)
        JW = at("JW", Z4 + 2560, [2 * DC, D], F16)
        JH = at("JH", Z4 + 5120, [2 * NT, D], F16)
        dsti2 = at("dsti2", Z4, [CHUNKS], I32)
        rowd = at("rowd", Z4 + 160, [ROWLEN], F32)
        DVD = at("DVD", dvb_at, [NT, P], F32)
        tot = at("tot", Z4 + 320, [4, STEPS + 2], F32)
        RDN = at("RDN", Z4 + 13568, [G], F32)

        bank = ctx.enter_context(nc.psum_tensor("bank", [P, 8, 512], F32))
        LNQ = [lnq[:, :], lnq1[:, :]]
        WSR = [WS[:, 0, :], WS[:, 1, :], WS3[:, :]]
        EX2 = [EX1[:, :], dvb[:, :]]
        bank16 = bank[:, :, :].rearrange("p b c -> p (b c)").bitcast(F16).rearrange("p (b c) -> p b c", b=8)

        pads_set = sem("pads_set")
        consts_set = sem("consts_set")
        consts2_set = sem("consts2_set")
        edges_in = sem("edges_in")
        x_in = sem("x_in")
        att_in = sem("att_in")
        wk_in = sem("wk_in")
        xT_in = sem("xT_in")
        gw_in = sem("gw_in")
        gpar_in = sem("gpar_in")
        counts_done = sem("counts_done")
        totals_done = sem("totals_done")
        ctl_set = sem("ctl_set")
        iota_wide = sem("iota_wide")
        window_set = sem("window_set")
        g_window_set = sem("g_window_set")
        onehots = sem("onehots")
        g_onehots = sem("g_onehots")
        g_onehots_used = sem("g_onehots_used")
        sub_counted = sem("sub_counted")
        sub_copied = sem("sub_copied")
        tposed = sem("tposed")
        tposed_out = sem("tposed_out")
        squares = sem("squares")
        degs_done = sem("degs_done")
        degs_out = sem("degs_out")
        ln_rowstd = sem("ln_rowstd")
        dv_diag = sem("dv_diag")
        dvb_set = sem("dvb_set")
        dvc_set = sem("dvc_set")
        ln_inv = sem("ln_inv")
        ln_added = sem("ln_added")
        ln_sqadded = sem("ln_sqadded")
        dv_spread = sem("dv_spread")
        norm_set = sem("norm_set")
        ln_std = sem("ln_std")
        bn_var = sem("bn_var")
        bn_std = sem("bn_std")
        wa_diag = sem("wa_diag")
        wa_spread = sem("wa_spread")
        wa_set = sem("wa_set")
        ln_rows = sem("ln_rows")
        h_rows = sem("h_rows")
        h_high = sem("h_high")
        h_low = sem("h_low")
        t_diag = sem("t_diag")
        t_spread = sem("t_spread")
        t_used = sem("t_used")
        mask_set = sem("mask_set")
        mask_used = sem("mask_used")
        pq_diag = sem("pq_diag")
        pq_spread = sem("pq_spread")
        pq_set = sem("pq_set")
        exps = sem("exps")
        att_f32 = sem("att_f32")
        att_high = sem("att_high")
        att_low = sem("att_low")
        agg_unit = sem("agg_unit")
        agg_out = sem("agg_out")
        rden_set = sem("rden_set")
        xpad_set = sem("xpad_set")
        sumsq_set = sem("sumsq_set")
        sumsq_done = sem("sumsq_done")
        wscale_set = sem("wscale_set")
        wk_scaled = sem("wk_scaled")
        wk_high = sem("wk_high")
        wk_low = sem("wk_low")
        k_abs = sem("k_abs")
        k_clip = sem("k_clip")
        k_sq = sem("k_sq")
        k_cubea = sem("k_cubea")
        k_cubeb = sem("k_cubeb")
        k_val = sem("k_val")
        k_silu = sem("k_silu")
        k_high = sem("k_high")
        k_low = sem("k_low")
        k_used = sem("k_used")
        kan_copied = sem("kan_copied")
        x1_out = sem("x1_out")
        ln_sum = sem("ln_sum")
        ln_dev = sem("ln_dev")
        ln_sqr = sem("ln_sqr")
        ln_var = sem("ln_var")
        ln_y = sem("ln_y")
        x_high = sem("x_high")
        x_low = sem("x_low")
        c9_set = sem("c9_set")
        cf_copied = sem("cf_copied")
        cf_set = sem("cf_set")
        xpads_zero = sem("xpads_zero")
        gw_high = sem("gw_high")
        gw_low = sem("gw_low")
        y_done = sem("y_done")
        y_high = sem("y_high")
        y_low = sem("y_low")
        z_done = sem("z_done")
        z_out = sem("z_out")
        bn_set = sem("bn_set")
        relu_set = sem("relu_set")
        xr_in = sem("xr_in")
        out_set = sem("out_set")
        stored = sem("stored")

        def each(ap, n):
            return bass.AP(ap.tensor, ap.offset, [ap.ap[0], [0, n], ap.ap[1]])

        def wide(ap, m):
            return bass.AP(ap.tensor, ap.offset, [ap.ap[0], ap.ap[1], [0, m]])

        block = ctx.enter_context(nc.Block())

        @block.sync
        def _(sp):
            sp.dma_start(dsti[:, :], dst_c).then_inc(edges_in, 16)
            sp.dma_start(srci[:, :], src_c).then_inc(edges_in, 16)
            sp.dma_start(rowi[0:ROWS, :], bass.AP(dst_flat.tensor, 0, [[ROWLEN, ROWS], [1, ROWLEN + 1]])
                         ).then_inc(edges_in, 16)
            sp.dma_start(Wat[:, :, :], W.rearrange("(c p) o -> p c o", p=P)).then_inc(att_in, 16)
            sp.dma_start(abc[:, :, :].rearrange("p a b -> p (a b)"), bass.AP(a.tensor, 0, [[0, P], [1, 2 * D]])
                         ).then_inc(att_in, 16)
            sp.wait_ge(pads_set, 1)
            sp.dma_start(hx[:, 0:NT - 1, :], x[0:(NT - 1) * P, :].rearrange("(t p) d -> p t d", p=P)).then_inc(x_in, 16)
            sp.dma_start(hx[0:TAIL, NT - 1, :], x[(NT - 1) * P:N, :]).then_inc(x_in, 16)
            for i in range(KB):
                if i >= 1:
                    sp.wait_ge(wk_in, 16 * i)
                sp.dma_start(WKf[:, i, :].rearrange("p (c o) -> p c o", c=DC),
                             wk[i * D:(i + 1) * D, :].rearrange("(c p) o -> p c o", p=P)).then_inc(wk_in, 16)
            sp.dma_start(gpar[:, :, :, :], gvec).then_inc(gpar_in, 16)
            sp.wait_ge(agg_unit, (DC + 1) * NG)
            sp.dma_start(XT[:, :, 0:N], xT.rearrange("(c p) n -> p c n", p=P)).then_inc(xT_in, 16)
            for l in range(LAYERS):
                if l > 0:
                    sp.wait_ge(gw_low, l)
                else:
                    sp.wait_ge(k_used, (NG - 1) * UNITS + RING + PAIR * 6)
                sp.dma_start(GWf[:, :, :], gwT[l].rearrange("(c p) o -> p c o", p=P)).then_inc(gw_in, 16)
                if l == 0:
                    sp.wait_ge(kan_copied, NG + 1)
                    sp.dma_start(x1_dram.rearrange("(c p) n -> p c n", p=P), XT[:, :, 0:N]).then_inc(x1_out, 16)
            sp.wait_ge(y_done, LAYERS * NT)
            sp.wait_ge(x1_out, 16)
            sp.dma_start(XR[:, :, 0:N], x1_dram.rearrange("(c p) n -> p c n", p=P)).then_inc(xr_in, 16)
            for c in range(DC):
                sp.wait_ge(out_set, c + 1)
                sp.dma_start(outT[c * P:(c + 1) * P, :], Z[:, c, 0:N]).then_inc(stored, 16)
            sp.wait_ge(stored, 16 * DC)

        @block.gpsimd
        def _(pool):
            nc.gpsimd.memset(hx[:, NT - 1, :], 0.0).then_inc(pads_set, 1)
            nc.gpsimd.iota(iota[:, :], pattern=[[1, HALF]], base=0, channel_multiplier=0,
                           allow_small_or_imprecise_dtypes=True).then_inc(consts_set, 1)
            nc.gpsimd.memset(ident[:, :], 0.0)
            pool.drain()
            nc.gpsimd.affine_select(out=ident[:, :], in_=ident[:, :], compare_op=ALU.not_equal, fill=1.0, base=0,
                                    pattern=[[-1, P]], channel_multiplier=1)
            pool.drain()
            nc.gpsimd.tensor_copy(ident16[:, :], ident[:, :]).then_inc(consts_set, 1)
            for t in range(NT):
                pool.wait_ge(h_high, t + 1)
                nc.gpsimd.tensor_tensor(hL[:, t, :], hx[:, t, :], hH[:, t, :], ALU.subtract).then_inc(h_low, 1)
            for j in range(NT):
                pool.wait_ge(att_high, j + 1)
                nc.gpsimd.tensor_tensor(AL[:, j, :], EX[:, j % 3, :], CT[:, j, :], ALU.subtract).then_inc(att_low, 1)
            for n in range(2 * KB):
                pool.wait_ge(wk_scaled, 2 * (n // 2) + 2)
                pool.wait_ge(wk_high, n + 1)
                part = slice(n % 2 * (BLK // 2), (n % 2 + 1) * (BLK // 2))
                nc.gpsimd.tensor_tensor(WKh[:, n // 2, 1, part], WSR[n % 3], WKh[:, n // 2, 0, part], ALU.subtract
                                        ).then_inc(wk_low, 1)
            pool.wait_ge(dvc_set, 1)
            pool.wait_ge(wk_low, 2 * KB)
            nc.gpsimd.tensor_tensor(DVD[:, :, :], each(ident[:, :], NT), wide(dvc[:, :], P), ALU.mult
                                    ).then_inc(dv_diag, 1)
            pool.wait_ge(agg_unit, (DC + 1) * NG)
            nc.gpsimd.memset(XT[:, :, N:NGP], 0.0).then_inc(xpad_set, 1)
            with pool.Fori(0, NG) as g:
                for u in range(SUNITS):
                    pool.wait_ge(k_sq, g * SUNITS + (u + 1))
                    nc.gpsimd.tensor_tensor(kd[:, u % 2, :], kd[:, u % 2, :], kb[:, u % 2, :], ALU.mult
                                            ).then_inc(k_cubeb, 1)
            def split_weights(l):
                pool.wait_ge(gw_high, l + 1)
                nc.gpsimd.tensor_tensor(GWL[:, :, :], GWf[:, :, :], GWH[:, :, :].bitcast(F32), ALU.subtract
                                        ).then_inc(gw_low, 1)

            pool.wait_ge(k_used, (NG - 1) * UNITS + RING + PAIR * 8)
            split_weights(0)
            pool.wait_ge(k_used, NG * UNITS + RING)
            nc.gpsimd.memset(XH[:, :, NGP:NP].bitcast(F32), 0.0).then_inc(xpads_zero, 1)
            nc.gpsimd.memset(XL[:, :, NGP:NP].bitcast(F32), 0.0).then_inc(xpads_zero, 1)

            for t in range(NT):
                pool.wait_ge(cf_copied, t + 1)
                d = CF[:, t, t * P:(t + 1) * P]
                nc.gpsimd.tensor_tensor(d, d.bitcast(F32), ident[:, :], ALU.add).then_inc(cf_set, 1)
            for l in range(1, LAYERS):
                pool.wait_ge(y_done, NT * l)
                split_weights(l)

        @block.scalar
        def _(act):
            act.wait_ge(wa_spread, 1)
            nc.scalar.copy(WAB[:, :, :], bank[:, 4:6, :]).then_inc(wa_set, 1)
            def copy_sub(t, half, n):
                act.wait_ge(sub_counted, n + 2)
                for s in range(2):
                    src = bank[s * SUB:(s + 1) * SUB, 2 * half:2 * half + 2, 0:HB]
                    dst = CT[half * SUB:(half + 1) * SUB, t:t + 1, s * HALF:(s + 1) * HALF]
                    ins = nc.scalar.copy(dst.rearrange("p a (b c) -> p (a b) c", b=2), src)
                ins.then_inc(sub_copied, 1)

            def statistics(t):
                act.wait_ge(x_in, 32)
                act.wait_ge(wa_set, 1)
                for i in range(2):
                    nc.scalar.activation(bank[:, 4 + i, :], hx[:, t + i, :], ACT.Identity, accum_out=mv[:, 0, t + i:t + i + 1])
                act.drain()
                nc.scalar.mul(mv[:, 1, t:t + 2], mv[:, 0, t:t + 2], -1.0 / D)
                act.drain()
                for i in range(2):
                    nc.scalar.activation(bank[:, 4 + i, :], hx[:, t + i, :], ACT.Square, bias=mv[:, 1, t + i:t + i + 1],
                                         accum_out=mv[:, 2, t + i:t + i + 1])
                act.drain()

            def activations(t):
                act.wait_ge(ln_rows, 1)
                for i in (t, t + 1):
                    nc.scalar.activation(hx[:, i, :], hx[:, i, :], ACT.Relu, bias=lnr[:, 1, i:i + 1],
                                         scale=lnr[:, 0, i:i + 1]).then_inc(h_rows, 1)
                for i in (t, t + 1):
                    act.wait_ge(h_rows, i + 1)
                    nc.scalar.copy(hH[:, i, :], hx[:, i, :]).then_inc(h_high, 1)

            for t in range(NT):
                if t < NT // 2:
                    statistics(2 * t)
                else:
                    activations(2 * t - NT)
                for half in range(2):
                    copy_sub(t, half, 2 * t + (half + 1))
                if t == NT // 2 - 1:
                    nc.scalar.activation(lnr[:, 0, :], mv[:, 2, :], ACT.Sqrt, bias=tiny[:, 1:2], scale=1.0 / D
                                         ).then_inc(ln_rowstd, 1)
                if t < KB:
                    act.wait_ge(wk_in, 16 * (t + 1))
                    nc.scalar.activation(bank[:, 4:8, :].rearrange("p b c -> p (b c)"), WKf[:, t, :], ACT.Square,
                                         accum_out=wss[:, t:t + 1]).then_inc(squares, 1)
                    act.wait_ge(squares, t + 1)
            for t in range(NT):
                for b in range(2):
                    act.wait_ge(tposed, 2 * t + b + 1)
                    nc.scalar.copy(C16[:, 5 * b:5 * b + 5, t * P:(t + 1) * P],
                                   bank16[:, 2 * (t % 2) + b, 0:5 * P].rearrange("p (s c) -> p s c", s=5)
                                   ).then_inc(tposed_out, 1)
            for s in range(NT):
                if s >= 2:
                    act.wait_ge(mask_used, s - 1)
                act.wait_ge(tposed_out, 2 * NT)
                act.wait_ge(t_used, 1)
                nc.scalar.activation(MSK[:, s % 2, :], C16[:, s, :], ACT.Sign).then_inc(mask_set, 1)
            act.wait_ge(degs_done, 1)
            nc.scalar.activation(dvc[:, :], bank[:, 0, 0:NT], ACT.Sqrt, bias=1.0).then_inc(degs_out, 1)
            act.wait_ge(sumsq_done, 1)
            nc.scalar.activation(wsc[:, 2:3], bank[:, 7, 0:1], ACT.Sqrt, bias=tiny[:, 0:1]).then_inc(norm_set, 1)
            nc.scalar.activation(mv[:, 0, 0:1], tiny[:, 0:1], ACT.Exp)
            act.wait_ge(pq_spread, 1)
            nc.scalar.copy(PQ[:, 0, :], bank[:, 0:3, :].rearrange("p b c -> p (b c)")[:, 0:NP])
            act.wait_ge(pq_spread, 2)
            nc.scalar.copy(PQ[:, 1, :], bank[:, 3:6, :].rearrange("p b c -> p (b c)")[:, 0:NP]).then_inc(pq_set, 1)
            act.wait_ge(pq_set, 1)
            act.wait_ge(h_low, NT)

            def exponentials(j):
                if j >= 3:
                    act.wait_ge(att_low, j - 2)
                if j >= 2:
                    act.wait_ge(att_f32, j - 1)
                nc.scalar.activation(EX[:, j % 3, :], PQ[:, 0, :], ACT.Exp, bias=mx[:, 4, j:j + 1])
                nc.scalar.activation(EX2[j % 2], PQ[:, 1, :], ACT.Exp, bias=mx[:, 5, j:j + 1]).then_inc(exps, 1)

            exponentials(0)
            for j in range(NT):
                if j + 1 < NT:
                    exponentials(j + 1)
                act.wait_ge(att_f32, j + 1)
                nc.scalar.copy(CT[:, j, :], EX[:, j % 3, :]).then_inc(att_high, 1)
            act.wait_ge(wscale_set, 1)
            act.wait_ge(att_f32, NT)
            for i in range(KB):
                for n in (2 * i, 2 * i + 1):
                    if n >= 3:
                        act.wait_ge(wk_low, n - 2)
                    part = slice(n % 2 * (BLK // 2), (n % 2 + 1) * (BLK // 2))
                    nc.scalar.mul(WSR[n % 3], WKf[:, i, part], wsc[:, 0:1]).then_inc(wk_scaled, 1)
                for n in (2 * i, 2 * i + 1):
                    act.wait_ge(wk_scaled, n + 1)
                    part = slice(n % 2 * (BLK // 2), (n % 2 + 1) * (BLK // 2))
                    nc.scalar.copy(WKh[:, i, 0, part], WSR[n % 3]).then_inc(wk_high, 1)

            nc.scalar.activation(mv[:, 1, 0:1], tiny[:, 0:1], ACT.Abs)
            act.wait_ge(agg_out, NG * DC)
            with act.Fori(0, NG) as g:
                def distance(u):
                    act.wait_ge(agg_out, NG * DC)
                    src = AGG[:, PAIR * (u % 2):PAIR * (u % 2) + PAIR, bass.ds(g * G, G)]
                    nc.scalar.activation(kv[:, u % 2, :].rearrange("p (c n) -> p c n", c=PAIR), src, ACT.Abs,
                                         bias=cen[:, u // 2:u // 2 + 1], scale=INV_STEP).then_inc(k_abs, 1)

                def high(u):
                    act.wait_ge(k_used, g * UNITS + (u + 1))
                    nc.scalar.copy(BHL[:, u % RING, 0, :, :], kc[u % 3].rearrange("p (c n) -> p c n", c=PAIR)
                                   ).then_inc(k_high, 1)

                distance(0)
                for u in range(SUNITS):
                    if u + 1 < SUNITS:
                        distance(u + 1)
                    if u >= 2:
                        act.wait_ge(k_val, g * SUNITS + (u - 1))
                        high(u - 2)
                    act.wait_ge(k_clip, g * SUNITS + (u + 1))
                    act.wait_ge(k_low, g * UNITS + (u + 1))
                    nc.scalar.activation(kc[u % 3], ka[:, u % 2, :], ACT.Square, scale=(1.0 / 6.0) ** 0.5)
                    nc.scalar.activation(kd[:, u % 2, :], kb[:, u % 2, :], ACT.Square, scale=(4.0 / 6.0) ** 0.5
                                         ).then_inc(k_sq, 1)
                for u in range(SUNITS, UNITS):
                    act.wait_ge(k_low, g * UNITS + (u + 1))
                    act.wait_ge(k_val, g * SUNITS + (u - 1))
                    high(u - 2)
                    src = AGG[:, PAIR * (u % 2):PAIR * (u % 2) + PAIR, bass.ds(g * G, G)]
                    nc.scalar.activation(kc[u % 3].rearrange("p (c n) -> p c n", c=PAIR), src, ACT.Silu
                                         ).then_inc(k_silu, 1)
                for u in range(SUNITS, UNITS):
                    act.wait_ge(k_silu, g * (UNITS - SUNITS) + (u - SUNITS + 1))
                    high(u)
            def deviation(g):
                act.wait_ge(ln_var, g + 1)
                if g >= 2:
                    act.wait_ge(ln_y, g - 1)
                nc.scalar.activation(rst[:, g % 2, :], bank[:, 6 + g % 2, 0:G], ACT.Sqrt, bias=tiny[:, 1:2],
                                     scale=1.0 / D).then_inc(ln_std, 1)

            def high_part(g):
                act.wait_ge(ln_y, g + 1)
                nc.scalar.activation(XH[:, :, g * G:(g + 1) * G], AGG[:, :, g * G:(g + 1) * G], ACT.Relu
                                     ).then_inc(x_high, 1)

            def squared(g):
                act.wait_ge(ln_dev, g + 1)
                if g >= 2:
                    act.wait_ge(ln_sqadded, g - 1)
                nc.scalar.activation(sq2[:, 1 - g % 2, :, :], AGG[:, :, g * G:(g + 1) * G], ACT.Square).then_inc(ln_sqr, 1)

            nc.scalar.activation(wsc[:, 3:4], tiny[:, 0:1], ACT.Sqrt)
            act.wait_ge(dv_spread, 1)
            nc.scalar.copy(dvb[:, :], bank[:, 5:8, :].rearrange("p b c -> p (b c)")[:, 0:NP]).then_inc(dvb_set, 1)
            squared(0)
            squared(1)
            act.wait_ge(gw_in, 16)
            act.wait_ge(k_used, (NG - 1) * UNITS + RING + PAIR * 7)
            nc.scalar.copy(GWH[:, :, :], GWf[:, :, :]).then_inc(gw_high, 1)
            deviation(0)
            deviation(1)
            act.wait_ge(k_used, NG * UNITS + RING)
            high_part(0)
            nc.scalar.copy(C9[:, :], C16[:, NT - 1, :]).then_inc(c9_set, 1)
            high_part(1)
            squared(2)
            deviation(2)

            def widen(t):
                act.wait_ge(c9_set, 1)
                act.wait_ge(x1_out, 16)
                act.wait_ge(ln_dev, NG)
                if t >= NT // 2:
                    act.wait_ge(cf_copied, t)
                src = C9[:, :] if t == NT - 1 else C16[:, t, :]
                nc.scalar.copy(CF[:, t, :], src).then_inc(cf_copied, 1)

            def feature_high(l, t):
                act.wait_ge(y_done, l * NT + (t + 1))
                nc.scalar.mul(YH[:, t, :], bank[:, t % YB, :], dvc[:, t:t + 1]).then_inc(y_high, 1)

            for t in range(EARLY):
                feature_high(0, t)
            high_part(NG - 1)
            for t in range(EARLY):
                widen(t)

            def layer(l, first, last):
                for t in range(EARLY if first else 0, NT):
                    if first:
                        widen(t)
                    feature_high(l, t)
                if not last:
                    act.wait_ge(gw_in, l * 16 + 32)
                    nc.scalar.copy(GWH[:, :, :], GWf[:, :, :]).then_inc(gw_high, 1)
                for c in range(DC):
                    act.wait_ge(bn_var, l * DC + (c + 1))
                    nc.scalar.activation(bnc[:, 2, c:c + 1], bnm[:, 1:2], ACT.Sqrt, bias=tiny[:, 1:2]).then_inc(bn_std, 1)
                    act.wait_ge(bn_set, l * DC + (c + 1))
                    nc.scalar.activation(Z[:, c, :], Z[:, c, :], ACT.Relu, bias=bnc[:, 1, c:c + 1],
                                         scale=bnc[:, 0, c:c + 1]).then_inc(relu_set, 1)
                    if not last:
                        act.wait_ge(relu_set, l * DC + (c + 1))
                        nc.scalar.copy(XH[:, c, 0:NGP], Z[:, c, :]).then_inc(x_high, 1)

            layer(0, True, False)
            with act.Fori(1, LAYERS - 1) as l:
                layer(l, False, False)
            layer(LAYERS - 1, False, True)

        @block.vector
        def _(dve):
            V = nc.vector

            def diagonals(out, cols, done):
                n = out.shape[1]
                V.tensor_tensor(out, each(ident[:, :], n), wide(cols, P), ALU.mult).then_inc(done, 1)

            V.memset(ones[:, :], 1.0)
            V.memset(ones16[:, :], 1.0)
            V.memset(zero16[:, :], 0.0)
            V.memset(cnt[:, :], 0.0)
            for p in range(SPL):
                V.memset(cen[:, p:p + 1], 0.5 * SPL - 0.5 - p)
            V.memset(tiny[:, 0:1], 1e-30)
            V.memset(tiny[:, 1:2], EPS)
            dve.drain()
            V.memset(wsc[:, :], 0.0).then_inc(consts2_set, 1)
            for i, (free, n) in enumerate(((sub_counted, 2), (g_onehots_used, 2), (sub_copied, 2), (k_used, RING),
                                           (k_low, 3), (kan_copied, 1), (y_low, YB), (z_out, YB))):
                V.memset(junk[:, i:i + 1], 0.0).then_inc(free, n)
            dve.wait_ge(edges_in, 48)
            V.tensor_copy(dstf[:, :], dsti[:, :])
            V.tensor_copy(srcm[:, :], srci[:, :])
            V.tensor_scalar(dsti2[:, :], dsti[:, :], 6, 6, ALU.arith_shift_right, ALU.arith_shift_left)
            V.tensor_copy(rowf[0:ROWS, :], rowi[0:ROWS, :])
            dve.drain()
            V.tensor_scalar(tmp[:, :], srcm[:, :], float(HALF), None, ALU.is_ge)
            V.tensor_copy(key[:, :], dsti2[:, :])
            V.tensor_tensor(rowd[0:ROWS, :], rowf[0:ROWS, 1:ROWLEN + 1], rowf[0:ROWS, 0:ROWLEN], ALU.subtract)
            dve.drain()
            V.tensor_tensor(key[:, :], key[:, :], dstf[:, :], ALU.add)
            V.scalar_tensor_tensor(srcm[:, :], tmp[:, :], -float(HALF), srcm[:, :], ALU.mult, ALU.add)
            V.tensor_scalar(junk[0:ROWS, :], rowd[0:ROWS, :], 0.0, None, ALU.is_lt, ALU.add,
                            accum_out=cnt[0:ROWS, STEPS + 1:STEPS + 2])
            dve.drain()
            V.scalar_tensor_tensor(key[:, :], tmp[:, :], float(SUB), key[:, :], ALU.mult, ALU.add)
            for d in range(1, STEPS + 1):
                ins = V.tensor_scalar(JC[:, d - 1, :], dstf[:, :], float(SUB * d), None, ALU.is_lt, ALU.add,
                                      accum_out=cnt[:, d:d + 1])
            ins.then_inc(counts_done, 1)
            dve.wait_ge(att_in, 32)
            for k in range(2):
                for c in range(DC):
                    V.tensor_tensor_reduce(out=JW[:, k * DC + c, :], in0=Wat[:, c, :], in1=abc[:, k, :], scale=1.0, scalar=0.0,
                                           op0=ALU.mult, op1=ALU.add, accum_out=wacol[:, k * DC + c:k * DC + c + 1])
            dve.drain()
            dve.wait_ge(consts_set, 2)
            diagonals(DG[:, 0, 0:2 * DC, :], wacol[:, :], wa_diag)
            dve.wait_ge(totals_done, 1)
            V.tensor_copy(tot[0:1, 0, :], bank[0:1, 0, 0:STEPS + 2])
            V.tensor_copy(ctl[0:1, 0:STEPS], bank[0:1, 0, 0:STEPS])
            dve.drain()
            V.tensor_scalar(ctl[0:1, 0:STEPS], ctl[0:1, 0:STEPS], 7, None, ALU.arith_shift_right)
            dve.drain()
            V.tensor_scalar(ctl[0:1, 0:STEPS], ctl[0:1, 0:STEPS], CHUNKS - WIN, None, ALU.min)
            dve.drain()
            V.tensor_copy(tot[0:1, 1, 0:STEPS], ctl[0:1, 0:STEPS])
            dve.drain()
            V.scalar_tensor_tensor(tot[0:1, 2, 0:STEPS], tot[0:1, 1, 0:STEPS], -float(P), tot[0:1, 0, 1:STEPS + 1],
                                   ALU.mult, ALU.add)
            dve.drain()
            V.tensor_scalar(tot[0:1, 2, 0:STEPS], tot[0:1, 2, 0:STEPS], float(WIN * P), 0.0, ALU.subtract, ALU.max)
            dve.drain()
            V.tensor_copy(tot[0:1, 2, STEPS:STEPS + 1], tot[0:1, 0, STEPS + 1:STEPS + 2])
            dve.drain()
            V.tensor_reduce(tot[0:1, 3, 0:1], tot[0:1, 2, 0:STEPS + 1], AX, ALU.add)
            dve.drain()
            V.tensor_copy(ctl[0:1, STEPS:STEPS + 1], tot[0:1, 3, 0:1]).then_inc(ctl_set, 1)
            dve.wait_ge(ctl_set, 1)
            dve.wait_ge(wa_spread, 1)

            V.tensor_scalar(koff[:, :], iota[:, 0:STEPS + 1], float(P), None, ALU.mult)
            V.tensor_copy(iotaw[:, :, :], wide(iota[:, 0:P], WIN)).then_inc(iota_wide, 1)
            dve.wait_ge(iota_wide, 1)

            def extract(first, step, buf, done):
                V.tensor_scalar(kwin[:, buf, :], key[:, bass.ds(first, WIN)], koff[:, bass.ds(step, 1)], None,
                                ALU.subtract)
                V.tensor_copy(swin[:, buf, :], srcm[:, bass.ds(first, WIN)]).then_inc(done, 1)

            def destination_rows(buf):
                V.tensor_tensor(OD[:, buf, :, :], iotaw[:, :, :], each(kwin[:, buf, :], P), ALU.is_equal)

            def source_rows(buf, k0, k1, ready):
                for k in range(k0, k1):
                    ins = V.tensor_scalar(OS[:, buf, k, :], iota[:, :], swin[:, buf, k:k + 1], None, ALU.is_equal)
                ins.then_inc(ready, 1)

            def row_scales():
                dve.wait_ge(ln_rowstd, 1)
                V.reciprocal(lnr[:, 0, :], lnr[:, 0, :])
                dve.drain()
                V.tensor_tensor(lnr[:, 1, :], mv[:, 1, :], lnr[:, 0, :], ALU.mult).then_inc(ln_rows, 1)

            bad = dve.value_load(ctl[0:1, STEPS:STEPS + 1], min_val=0, max_val=1 << 20)
            with dve.If(bad > 0):
                def every_window(d):
                    with dve.Fori(0, WINDOWS // 2) as w:
                        for buf in range(2):
                            n = (d * (WINDOWS // 2) + w) * 2 + buf
                            dve.wait_ge(g_onehots_used, n + 1)
                            extract(w * (2 * WIN) + buf * WIN, d, buf, g_window_set)
                            dve.wait_ge(g_window_set, n + 1)
                            destination_rows(buf)
                            source_rows(buf, 0, WIN // 2, g_onehots)
                            source_rows(buf, WIN // 2, WIN, g_onehots)

                with dve.Fori(0, STEPS // 2) as d:
                    every_window(d)
                row_scales()
                with dve.Fori(STEPS // 2, STEPS) as d:
                    every_window(d)
                dve.nop()
            with dve.Else():
                extract(dve.value_load(ctl[0:1, 0:1], min_val=0, max_val=CHUNKS - WIN), 0, 0, window_set)
                def one_window(t):
                    for half in range(2):
                        dve.wait_ge(sub_counted, t * 2 + (half + 1))
                        dve.wait_ge(window_set, t * 2 + (half + 1))
                        destination_rows(half)
                        source_rows(half, 0, WIN // 2, onehots)
                        first = dve.value_load(ctl[0:1, bass.ds(t * 2 + (half + 1), 1)], min_val=0, max_val=CHUNKS - WIN)
                        dve.drain()
                        extract(first, t * 2 + (half + 1), 1 - half, window_set)
                        source_rows(half, WIN // 2, WIN, onehots)

                with dve.Fori(0, NT // 2) as t:
                    one_window(t)
                row_scales()
                with dve.Fori(NT // 2, NT) as t:
                    one_window(t)
                dve.nop()

            dve.wait_ge(wa_set, 1)
            dve.wait_ge(sub_counted, STEPS + 2)
            for k in (1, 0):
                for t in range(NT):
                    dve.wait_ge(h_rows, t + 1)
                    V.tensor_tensor_reduce(out=JH[:, 2 * t + k, :], in0=hx[:, t, :], in1=WAB[:, k, :], scale=1.0, scalar=0.0,
                                           op0=ALU.mult, op1=ALU.add, accum_out=st[:, k, t:t + 1])
                dve.drain()
                if k == 1:
                    diagonals(DG2[:, :, :], st[:, 1, :], t_diag)
            dve.wait_ge(squares, KB)
            V.tensor_reduce(wsc[:, 0:1], wss[:, :], AX, ALU.add).then_inc(sumsq_set, 1)
            V.tensor_copy(mx[:, 4, :], st[:, 1, :])
            V.tensor_scalar(mx[:, 5, :], st[:, 1, :], LEAK, None, ALU.mult)
            dve.wait_ge(t_spread, 1)
            trow = bank[:, 5:8, :].rearrange("p b c -> p (b c)")[:, 0:NP]
            V.tensor_reduce(tmin[:, 0:1], trow, AX, ALU.min)
            dve.drain()
            V.tensor_scalar(tmin[:, 1:2], tmin[:, 0:1], 1.0, None, ALU.subtract)
            dve.drain()
            V.tensor_scalar(U[:, :], trow, tmin[:, 1:2], None, ALU.subtract).then_inc(t_used, 1)
            dve.wait_ge(tposed_out, 2 * NT)
            for s in range(NT):
                dve.wait_ge(mask_set, s + 1)
                dve.drain()
                V.tensor_tensor_reduce(out=SCR[:, :], in0=MSK[:, s % 2, :], in1=U[:, :], scale=1.0, scalar=0.0,
                                       op0=ALU.mult, op1=ALU.max, accum_out=mx[:, 0, s:s + 1]).then_inc(mask_used, 1)
            dve.drain()
            V.scalar_tensor_tensor(mx[:, 0, :], mx[:, 0, :], tmin[:, 1:2], st[:, 0, :], ALU.add, ALU.add)
            dve.drain()
            V.scalar_tensor_tensor(mx[:, 1, :], mx[:, 0, :], LEAK, mx[:, 0, :], ALU.mult, ALU.max)
            dve.drain()
            V.tensor_tensor(mx[:, 2, :], st[:, 0, :], mx[:, 1, :], ALU.subtract)
            V.scalar_tensor_tensor(mx[:, 3, :], st[:, 0, :], LEAK, mx[:, 1, :], ALU.mult, ALU.subtract)
            dve.drain()
            for k in range(2):
                diagonals(DG[:, k, :, :], mx[:, 2 + k, :], pq_diag)
            dve.wait_ge(norm_set, 1)
            V.reciprocal(wsc[:, 1:2], wsc[:, 2:3])
            dve.drain()
            V.tensor_scalar(wsc[:, 1:2], wsc[:, 1:2], 16384.0, None, ALU.mult)
            dve.drain()
            V.tensor_scalar(wsc[:, 0:1].bitcast(I32), wsc[:, 1:2].bitcast(I32), 0x7F800000, None, ALU.bitwise_and)
            dve.drain()
            V.reciprocal(wsc[:, 1:2], wsc[:, 0:1]).then_inc(wscale_set, 1)
            dve.wait_ge(degs_out, 1)
            V.reciprocal(dvc[:, :], dvc[:, :]).then_inc(dvc_set, 1)
            for j in range(NT):
                dve.wait_ge(exps, j + 1)
                V.tensor_tensor(EX[:, j % 3, :], EX[:, j % 3, :], EX2[j % 2], ALU.max)
                dve.drain()
                V.scalar_tensor_tensor(EX[:, j % 3, :], EX[:, j % 3, :], 1.0, CT[:, j, :], ALU.min, ALU.mult
                                       ).then_inc(att_f32, 1)
            for g in range(NG):
                u = (DC + 1) * g
                dve.wait_ge(agg_unit, u + 1)
                dve.drain()
                V.tensor_scalar(RDN[:, :], bank[:, u % 8, 0:G], 1e-30, None, ALU.max)
                dve.drain()
                V.reciprocal(RDN[:, :], RDN[:, :]).then_inc(rden_set, 1)
                dve.wait_ge(rden_set, g + 1)
                for c in range(DC):
                    dve.wait_ge(agg_unit, u + 2 + c)
                    V.tensor_tensor(AGG[:, c, g * G:(g + 1) * G], bank[:, (u + 1 + c) % 8, 0:G], RDN[:, :], ALU.mult
                                    ).then_inc(agg_out, 1)

            dve.wait_ge(agg_unit, (DC + 1) * NG)

            def low(g, u):
                dve.wait_ge(k_high, g * UNITS + (u + 1))
                V.tensor_tensor(BHL[:, u % RING, 1, :, :].rearrange("p c n -> p (c n)"), kc[u % 3],
                                BHL[:, u % RING, 0, :, :].rearrange("p c n -> p (c n)"), ALU.subtract).then_inc(k_low, 1)

            def turn(g, u):
                v = (u - 1) % 2
                if u < SUNITS:
                    dve.wait_ge(k_abs, g * SUNITS + (u + 1))
                    V.tensor_scalar(ka[:, u % 2, :], kv[:, u % 2, :], 2.0, 2.0, ALU.min, ALU.subtract)
                    V.tensor_scalar(kb[:, u % 2, :], kv[:, u % 2, :], 1.0, 1.0, ALU.min, ALU.subtract
                                    ).then_inc(k_clip, 1)
                if u >= 1:
                    dve.wait_ge(k_sq, g * SUNITS + u)
                    V.tensor_tensor(kc[(u - 1) % 3], kc[(u - 1) % 3], ka[:, v, :], ALU.mult).then_inc(k_cubea, 1)
                if u >= 2:
                    low(g, u - 2)
                if u >= 1:
                    dve.wait_ge(k_cubea, g * SUNITS + u)
                    dve.wait_ge(k_cubeb, g * SUNITS + u)
                    V.tensor_tensor(kc[(u - 1) % 3], kd[:, v, :], kc[(u - 1) % 3], ALU.subtract).then_inc(k_val, 1)

            def copied(g):
                dve.wait_ge(k_used, g * UNITS + (UNITS + RING))
                dve.wait_ge(xT_in, 16)
                dve.wait_ge(xpad_set, 1)
                for c in range(DC):
                    xc = XT[:, c, bass.ds(g * G, G)]
                    ins = V.scalar_tensor_tensor(xc, bank[:, c, 0:G], wsc[:, 1:2], xc, ALU.mult, ALU.add)
                ins.then_inc(kan_copied, 1)

            def group(g, last):
                for u in range(AHEAD, SUNITS + 1):
                    turn(g, u)
                for u in range(SUNITS - 1, UNITS):
                    low(g, u)
                if not last:
                    for u in range(AHEAD):
                        turn(g + 1, u)
                if not last:
                    copied(g)

            for u in range(AHEAD):
                turn(0, u)
            with dve.Fori(0, NG - 1) as g:
                group(g, False)
            group(NG - 1, True)

            def chunk_sum(out, src, done):
                V.tensor_tensor(out, src[:, 0, :], src[:, 1, :], ALU.add)
                V.tensor_tensor(lnp[:, :], src[:, 2, :], src[:, 3, :], ALU.add)
                dve.drain()
                V.tensor_tensor(out, out, lnp[:, :], ALU.add).then_inc(done, 1)
                dve.drain()

            def added(g):
                if g >= 2:
                    dve.wait_ge(ln_sum, g - 1)
                chunk_sum(lnx[:, g % 2, :], XT[:, :, g * G:(g + 1) * G], ln_added)

            def centered(g):
                dve.wait_ge(ln_sum, g + 1)
                for c in range(DC):
                    ins = V.scalar_tensor_tensor(AGG[:, c, g * G:(g + 1) * G], bank[:, 4 + g % 2, 0:G], -1.0 / D,
                                                 XT[:, c, g * G:(g + 1) * G], ALU.mult, ALU.add)
                ins.then_inc(ln_dev, 1)

            def squares_added(g):
                dve.wait_ge(ln_sqr, g + 1)
                if g >= 2:
                    dve.wait_ge(ln_var, g - 1)
                chunk_sum(LNQ[g % 2], sq2[:, 1 - g % 2, :, :], ln_sqadded)

            def inverse(g):
                dve.wait_ge(ln_std, g + 1)
                V.reciprocal(rst[:, g % 2, :], rst[:, g % 2, :]).then_inc(ln_inv, 1)

            def normalized(g):
                dve.wait_ge(ln_inv, g + 1)
                for c in range(DC):
                    y = AGG[:, c, g * G:(g + 1) * G]
                    ins = V.tensor_tensor(y, y, rst[:, g % 2, :], ALU.mult)
                ins.then_inc(ln_y, 1)

            def split_low(g):
                dve.wait_ge(x_high, g + 1)
                y = slice(g * G, (g + 1) * G)
                V.scalar_tensor_tensor(XL[:, :, y], AGG[:, :, y], 0.0, XH[:, :, y].bitcast(F32), ALU.max, ALU.subtract
                                       ).then_inc(x_low, 1)

            def feature_low(l, t):
                dve.wait_ge(y_high, l * NT + (t + 1))
                V.scalar_tensor_tensor(YL[:, t, :], bank[:, t % YB, :], dvc[:, t:t + 1], YH[:, t, :].bitcast(F32),
                                       ALU.mult, ALU.subtract).then_inc(y_low, 1)

            dve.wait_ge(kan_copied, NG)
            added(0)
            added(1)
            centered(0)
            centered(1)
            squares_added(0)
            squares_added(1)
            inverse(0)
            normalized(0)
            inverse(1)
            copied(NG - 1)
            dve.wait_ge(kan_copied, NG + 1)
            split_low(0)
            added(2)
            normalized(1)
            centered(2)
            split_low(1)
            squares_added(2)
            inverse(2)
            for t in range(EARLY):
                feature_low(0, t)
            normalized(2)
            split_low(2)

            dve.wait_ge(gpar_in, 16)

            def finish(l, c, last):
                if last:
                    dve.wait_ge(xr_in, 16)
                    dve.wait_ge(relu_set, l * DC + (c + 1))
                    V.tensor_tensor(Z[:, c, 0:N], Z[:, c, 0:N], XR[:, c, 0:N], ALU.add).then_inc(out_set, 1)
                else:
                    dve.wait_ge(x_high, l * DC + (NG + c + 1))
                    V.tensor_tensor(XL[:, c, 0:NGP], Z[:, c, :], XH[:, c, 0:NGP].bitcast(F32), ALU.subtract
                                    ).then_inc(x_low, 1)

            def layer(l, first, last):
                for t in range(EARLY if first else 0, NT):
                    feature_low(l, t)
                for c in range(DC):
                    for g in range(NG):
                        u = c * NG + g
                        dve.wait_ge(z_done, l * (DC * NG) + (u + 1))
                        V.tensor_tensor(Z[:, c, g * G:(g + 1) * G], bank[:, YB + u % YB, 0:G],
                                        dvb[:, g * G:(g + 1) * G], ALU.mult).then_inc(z_out, 1)
                        dve.drain()
                        V.bn_stats(bnz[:, g, :], Z[:, c, g * G:min((g + 1) * G, N)])
                    dve.drain()
                    V.bn_aggr(bnm[:, :], bnz[:, :, :]).then_inc(bn_var, 1)
                    dve.wait_ge(bn_std, l * DC + (c + 1))
                    b, gamma, beta = (gpar[:, k, bass.ds(l, 1), c] for k in range(3))
                    V.reciprocal(bnc[:, 2, c:c + 1], bnc[:, 2, c:c + 1])
                    V.tensor_tensor(bnc[:, 3, c:c + 1], bnm[:, 0:1], b, ALU.add)
                    dve.drain()
                    V.tensor_tensor(bnc[:, 0, c:c + 1], bnc[:, 2, c:c + 1], gamma, ALU.mult)
                    V.tensor_tensor(bnc[:, 3, c:c + 1], b, bnc[:, 3, c:c + 1], ALU.subtract)
                    dve.drain()
                    V.scalar_tensor_tensor(bnc[:, 1, c:c + 1], bnc[:, 3, c:c + 1], bnc[:, 0, c:c + 1], beta,
                                           ALU.mult, ALU.add).then_inc(bn_set, 1)
                    if c >= 1:
                        finish(l, c - 1, last)
                finish(l, DC - 1, last)

            layer(0, True, False)
            with dve.Fori(1, LAYERS - 1) as l:
                layer(l, False, False)
            layer(LAYERS - 1, False, True)

        @block.tensor
        def _(pe):
            mm = nc.tensor.matmul
            pe.wait_ge(consts2_set, 1)
            pe.wait_ge(counts_done, 1)
            mm(bank[0:1, 0, 0:STEPS + 2], ones[:, 0:1], cnt[:, :], start=True, stop=True).then_inc(totals_done, 1)

            def spread(b0, dg, n, done=None):
                for i in range(n):
                    ins = mm(bank[:, b0 + i // 4, (i % 4) * P:(i % 4 + 1) * P], ones[:, :], dg[:, i, :],
                             start=True, stop=True)
                if done is not None:
                    ins.then_inc(done, 1)

            pe.wait_ge(wa_diag, 1)
            spread(4, DG[:, 0, :, :], 2 * DC, wa_spread)
            pe.wait_ge(ctl_set, 1)

            def count(half, buf, n, ready, used, start, stop):
                for k in range(WIN):
                    if k % (WIN // 2) == 0:
                        pe.wait_ge(ready, n * 2 + (k // (WIN // 2) + 1))
                    for b in range(2):
                        ins = mm(bank[:, 2 * half + b, 0:HB], OD[:, buf, :, k], OS[:, buf, k, b * HB:(b + 1) * HB],
                                 start=(start and k == 0), stop=(stop and k == WIN - 1))
                return ins.then_inc(used, 1)

            bad = pe.value_load(ctl[0:1, STEPS:STEPS + 1], min_val=0, max_val=1 << 20)
            with pe.If(bad > 0):
                with pe.Fori(0, NT) as t:
                    for half in range(2):
                        pe.wait_ge(sub_copied, t * 2 + (half + 1))
                        for b in range(2):
                            mm(bank[:, 2 * half + b, 0:HB], ones16[:, :], zero16[:, :], start=True, stop=False)
                        with pe.Fori(0, WINDOWS // 2) as w:
                            for buf in range(2):
                                n = ((t * 2 + half) * (WINDOWS // 2) + w) * 2 + buf
                                count(half, buf, n, g_onehots, g_onehots_used, False, False)
                        for b in range(2):
                            ins = mm(bank[:, 2 * half + b, 0:HB], ones16[:, :], zero16[:, :], start=False, stop=True)
                        ins.then_inc(sub_counted, 1)
                pe.nop()
            with pe.Else():
                with pe.Fori(0, NT) as t:
                    for half in range(2):
                        pe.wait_ge(sub_copied, t * 2 + (half + 1))
                        count(half, half, t * 2 + half, onehots, sub_counted, True, True)
                pe.nop()

            pe.wait_ge(sub_copied, 2 + STEPS)
            for t in range(NT):
                for b in range(2):
                    if t >= 2:
                        pe.wait_ge(tposed_out, 2 * t + b - 3)
                    for s in range(5):
                        ins = nc.tensor.transpose(bank16[:, 2 * (t % 2) + b, s * P:(s + 1) * P],
                                                  CT[:, t, (5 * b + s) * P:(5 * b + s + 1) * P], ident16[:, :])
                    ins.then_inc(tposed, 1)
                if t == NT // 2:
                    pe.wait_ge(t_diag, 1)
                    pe.wait_ge(squares, KB)
                    spread(5, DG2, NT, t_spread)
            pe.wait_ge(tposed_out, 2 * NT)
            for t in range(NT):
                for s in range(NT):
                    ins = mm(bank[:, 0, t:t + 1], C16[:, s, t * P:(t + 1) * P], ones16[:, 0:1], start=(s == 0),
                             stop=(s == NT - 1))
            ins.then_inc(degs_done, 1)
            pe.wait_ge(sumsq_set, 1)
            pe.wait_ge(t_used, 1)
            mm(bank[:, 7, 0:1], ones[:, :], wsc[:, 0:1], start=True, stop=True).then_inc(sumsq_done, 1)
            pe.wait_ge(pq_diag, 1)
            pe.wait_ge(degs_out, 1)
            spread(0, DG[:, 0, :, :], NT, pq_spread)
            pe.wait_ge(pq_diag, 2)
            spread(3, DG[:, 1, :, :], NT, pq_spread)

            def attend(g, k, j):
                cols = slice(g * G, (g + 1) * G)
                if k == 0:
                    parts = [(ones16[:, :], CT), (ones16[:, :], AL)]
                else:
                    fh, fl = (h[:, j, (k - 1) * P:k * P] for h in (hH, hL))
                    parts = [(fh, CT), (fh, AL), (fl, CT)]
                for i, (lhs, m) in enumerate(parts):
                    ins = mm(bank[:, ((DC + 1) * g + k) % 8, 0:G], lhs, m[:, j, cols],
                             start=(j == 0 and i == 0), stop=(j == NT - 1 and i == len(parts) - 1))
                if j == NT - 1:
                    ins.then_inc(agg_unit, 1)

            pe.wait_ge(h_low, NT)
            pe.wait_ge(pq_set, 1)
            for j in range(NT):
                pe.wait_ge(att_low, j + 1)
                for unit in range(8):
                    attend(*divmod(unit, DC + 1), j)
            for unit in range(8, NG * (DC + 1)):
                pg, pk = divmod(unit - 8, DC + 1)
                if pk == 0:
                    pe.wait_ge(rden_set, pg + 1)
                else:
                    pe.wait_ge(agg_out, DC * pg + pk)
                for j in range(NT):
                    attend(*divmod(unit, DC + 1), j)

            pe.wait_ge(agg_out, DC * NG)
            pe.wait_ge(dv_diag, 1)
            spread(5, DVD, NT, dv_spread)
            pe.wait_ge(wk_low, 2 * KB)

            def means(g):
                pe.wait_ge(ln_added, g + 1)
                if g >= 2:
                    pe.wait_ge(ln_dev, g - 1)
                mm(bank[:, 4 + g % 2, 0:G], ones[:, :], lnx[:, g % 2, :], start=True, stop=True).then_inc(ln_sum, 1)

            def variances(g):
                pe.wait_ge(ln_sqadded, g + 1)
                if g >= 2:
                    pe.wait_ge(ln_std, g - 1)
                mm(bank[:, 6 + g % 2, 0:G], ones[:, :], LNQ[g % 2], start=True, stop=True).then_inc(ln_var, 1)

            def units(g, last):
                for u in range(UNITS):
                    pe.wait_ge(k_low, g * UNITS + (u + 4))
                    if u == 0:
                        pe.wait_ge(kan_copied, g + 1)
                    for o in range(DC):
                        for q in range(PAIR):
                            wcol = (PAIR * (u % 2) + q) * D + o * P
                            wh, wl = (WKh[:, u // 2, i, wcol:wcol + P] for i in range(2))
                            bh, bl = (BHL[:, u % RING, i, q, :] for i in range(2))
                            for i, (lhs, rhs) in enumerate(((wh, bh), (wh, bl), (wl, bh))):
                                ins = mm(bank[:, o, 0:G], lhs, rhs, start=(u == 0 and q == 0 and i == 0),
                                         stop=(u == UNITS - 1 and q == PAIR - 1 and i == 2))
                    ins.then_inc(k_used, 1)

                    if last and u == UNITS - 5:
                        pe.wait_ge(dvb_set, 1)
                        means(0)
                        means(1)
                    if last and u == UNITS - 3:
                        variances(0)
                        variances(1)

            with pe.Fori(0, NG - 1) as g:
                units(g, False)
            units(NG - 1, True)
            means(2)

            pe.wait_ge(xpads_zero, 2)
            pe.wait_ge(kan_copied, NG + 1)

            def feature(t, c):
                xh, xl = (X[:, c, t * P:(t + 1) * P] for X in (XH, XL))
                for i, (lhs, rhs) in enumerate(((xh, GWH), (xh, GWL), (xl, GWH))):
                    ins = mm(bank[:, t % YB, :], lhs, rhs[:, c, :], start=(c == 0 and i == 0),
                             stop=(c == DC - 1 and i == 2))
                if c == DC - 1:
                    ins.then_inc(y_done, 1)

            def layer(l, first):
                pe.wait_ge(gw_low, l + 1)
                if not first:
                    pe.wait_ge(y_low, l * NT + YB)
                    for c in range(DC):
                        pe.wait_ge(x_low, (l - 1) * DC + (NG + c + 1))
                        for t in range(YB):
                            feature(t, c)
                for t in range(0 if first else YB, NT):
                    pe.wait_ge(y_low, l * NT + (t + 1))
                    if first:
                        pe.wait_ge(x_low, min(NG, -(-(t + 1) * P // G)))
                    for c in range(DC):
                        feature(t, c)
                    if first and t == 0:
                        variances(NG - 1)
                for o in range(DC):
                    for g in range(NG):
                        u = o * NG + g
                        pe.wait_ge(z_out, l * (DC * NG) + (u + 1))
                        for j in range(NT):
                            if u == 0:
                                pe.wait_ge(y_low, l * NT + (YB + j + 1))
                                pe.wait_ge(cf_set, j + 1)
                            for i, Y in enumerate((YH, YL)):
                                ins = mm(bank[:, YB + u % YB, 0:G], Y[:, j, o * P:(o + 1) * P],
                                         CF[:, j, g * G:(g + 1) * G], start=(j == 0 and i == 0),
                                         stop=(j == NT - 1 and i == 1))
                        ins.then_inc(z_done, 1)

            layer(0, True)
            with pe.Fori(1, LAYERS) as l:
                layer(l, False)


_ORDER = ["x", "xT", "src_c", "dst_c", "dst_flat", "W", "a", "wk", "gwT", "gvec"]


def kernel(**inputs):
    import numpy as np
    import concourse.bacc as bacc
    from concourse.bass_utils import run_bass_kernel_spmd

    i = {k: np.asarray(v) for k, v in inputs.items()}
    src = np.pad(i["src"], (0, EP - E))
    dst = np.pad(i["dst"], (0, EP - E), constant_values=NO_NODE)
    arrays = {
        "x": i["x"],
        "xT": i["x"].T,
        "src_c": src.reshape(CHUNKS, P).T,
        "dst_c": dst.reshape(CHUNKS, P).T,
        "dst_flat": dst,
        "W": i["L0_gnn_W"],
        "a": i["L0_gnn_a"].reshape(-1),
        "wk": np.concatenate([i["L0_gnn_spline_w"].transpose(2, 1, 0).reshape(SPL * D, D), i["L0_gnn_base_w"].T]),
        "gwT": i["L1_gnn_W"].transpose(0, 2, 1),
        "gvec": np.stack([i["L1_gnn_b"], i["L1_gnn_gamma"], i["L1_gnn_beta"]]).reshape(3, LAYERS, DC, P
                                                                                     ).transpose(3, 0, 1, 2),
    }
    arrays = {k: np.ascontiguousarray(v) for k, v in arrays.items()}
    nc = bacc.Bacc("TRN2", target_bir_lowering=False, num_devices=1)
    aps = [nc.dram_tensor(f"in_{k}", arrays[k].shape, mybir.dt.from_np(arrays[k].dtype), kind="ExternalInput").ap()
           for k in _ORDER]
    out = nc.dram_tensor("outT", (D, N), F32, kind="ExternalOutput").ap()
    build(nc, *aps, out)
    r = run_bass_kernel_spmd(nc, [{f"in_{k}": v for k, v in arrays.items()}], core_ids=[0])
    return np.ascontiguousarray(r.results[0]["outT"].T)
```
